# Optimizing a Trainium2 kernel written in Bass

```python
import numpy as np
import jax
import jax.numpy as jnp

def _softmax(x, axis=-1):
    return jax.nn.softmax(x, axis=axis)

def _gelu(x):
    return jax.nn.gelu(x, approximate=True)

def _silu(x):
    return jax.nn.silu(x)

def _sigmoid(x):
    return jax.nn.sigmoid(x)

def _layernorm(x, axis=-1, eps=1e-05):
    m = jnp.mean(x, axis=axis, keepdims=True)
    v = jnp.var(x, axis=axis, keepdims=True)
    return (x - m) / jnp.sqrt(v + eps)

def _scatter_add(tgt, idx, src, axis=0):
    return tgt.at[idx].add(src)

def _segment_sum(src, seg, n):
    return jax.ops.segment_sum(src, seg, n)
kernel_name = 'mk_adj_preln_d2_adj_r2_c84d4b'

def setup_inputs(seed: int=0):
    np.random.seed(seed)
    _w = jnp.asarray

    def _rec_inputs():
        import jax
        import jax.numpy as jnp
        _gk = jax.random.key(seed)
        x = -9.806e-05 + 1 * jax.random.normal(jax.random.fold_in(_gk, 1), (4096, 128), jnp.float32)
        _a = jax.random.bernoulli(jax.random.fold_in(_gk, 2), 0.00390625, (4096, 4096))
        _a = jnp.logical_or(_a, jnp.swapaxes(_a, -1, -2))
        _a = jnp.logical_or(_a, jnp.eye(4096, dtype=bool))
        _af = _a.astype(jnp.float32)
        _af = _af * jax.random.uniform(jax.random.fold_in(_gk, 3), (4096, 4096), jnp.float32, 0.05, 1)
        adj = _af
        return (x, adj)
    x, adj = _rec_inputs()

    def _L0_gnn_setup():
        import jax, jax.numpy as jnp
        import numpy as np

        def _lap_mul(A, x):
            d = 1.0 / jnp.sqrt(jnp.sum(A, axis=-1))
            return d[:, None] * (A @ (d[:, None] * x))
        key = jax.random.key(seed)
        k1, k2, k3, k4, k5, k6 = jax.random.split(key, 6)
        N, D_IN, D_OUT = (2048, 128, 128)
        x = jax.random.normal(k1, (N, D_IN), dtype=jnp.float32)
        A = jax.random.uniform(k2, (N, N), dtype=jnp.float32)
        s1 = 1.0 / np.sqrt(D_IN)
        W1 = jax.random.uniform(k3, (D_IN, D_OUT), minval=-s1, maxval=s1, dtype=jnp.float32)
        b1 = jax.random.uniform(k4, (D_OUT,), minval=-s1, maxval=s1, dtype=jnp.float32)
        W2 = jax.random.uniform(k5, (D_IN, D_OUT), minval=-s1, maxval=s1, dtype=jnp.float32)
        b2 = jax.random.uniform(k6, (D_OUT,), minval=-s1, maxval=s1, dtype=jnp.float32)
        return {'x': x, 'A': A, 'W1': W1, 'b1': b1, 'W2': W2, 'b2': b2, 'sigma': 1, 'k': 4}
    _L0_gnn_all = _L0_gnn_setup()
    _L0_gnn_in = {k: v for k, v in _L0_gnn_all.items() if k in ('W1', 'b1', 'W2', 'b2')}
    del _L0_gnn_all

    def _L1_gnn_setup():
        import jax, jax.numpy as jnp
        import numpy as np
        N = 8192
        F_IN = 128
        F_OUT = 128
        key = jax.random.key(seed)
        k1, k2, k3, k4 = jax.random.split(key, 4)
        x = jax.random.normal(k1, (N, F_IN), dtype=jnp.float32)
        adj = jax.random.uniform(k2, (N, N), dtype=jnp.float32)
        bound = 1.0 / np.sqrt(2 * F_IN)
        W = jax.random.uniform(k3, (F_OUT, 2 * F_IN), minval=-bound, maxval=bound, dtype=jnp.float32)
        b = jax.random.uniform(k4, (F_OUT,), minval=-bound, maxval=bound, dtype=jnp.float32)
        return {'x': x, 'adj': adj, 'W': W, 'b': b}
    _L1_gnn_all = _L1_gnn_setup()
    _L1_gnn_in = {k: v for k, v in _L1_gnn_all.items() if k in ('W', 'b')}
    del _L1_gnn_all
    return {'x': x, 'adj': adj, 'L0_gnn_W1': _L0_gnn_in['W1'], 'L0_gnn_b1': _L0_gnn_in['b1'], 'L0_gnn_W2': _L0_gnn_in['W2'], 'L0_gnn_b2': _L0_gnn_in['b2'], 'L1_gnn_W': _L1_gnn_in['W'], 'L1_gnn_b': _L1_gnn_in['b']}

def reference(x, adj, L0_gnn_W1, L0_gnn_b1, L0_gnn_W2, L0_gnn_b2, L1_gnn_W, L1_gnn_b):
    import jax
    import jax.numpy as jnp

    def _L0_gnn_ref(x, A, W1, b1, W2, b2, sigma, k):
        import jax, jax.numpy as jnp
        import numpy as np

        def _lap_mul(A, x):
            d = 1.0 / jnp.sqrt(jnp.sum(A, axis=-1))
            return d[:, None] * (A @ (d[:, None] * x))
        z = _lap_mul(A, x) @ W1 + b1
        z = jax.nn.leaky_relu(z, negative_slope=0.1)
        sq = jnp.sum(z * z, axis=-1)
        d2 = sq[:, None] + sq[None, :] - 2.0 * (z @ z.T)
        d2 = jnp.maximum(d2, 0.0)
        S = jnp.sqrt(d2 + 1e-10)
        S = jnp.exp(-S / (2.0 * sigma))
        order = jnp.argsort(-S, axis=-1)
        ranks = jnp.argsort(order, axis=-1)
        S = jnp.where(ranks < k, S, 0.0)
        A2 = S + A
        out = _lap_mul(A2, x) @ W2 + b2
        return out

    def _L1_gnn_ref(x, adj, W, b):
        import jax, jax.numpy as jnp
        import numpy as np
        N = 8192
        F_IN = 128
        F_OUT = 128
        neigh = adj @ x
        W_self = W[:, :F_IN]
        W_neigh = W[:, F_IN:]
        return x @ W_self.T + neigh @ W_neigh.T + b
    h = jnp.maximum(_layernorm(x, axis=-1), 0.0)
    x = x + _L0_gnn_ref(h, adj, L0_gnn_W1, L0_gnn_b1, L0_gnn_W2, L0_gnn_b2, 1, 4)
    h = jnp.maximum(_layernorm(x, axis=-1), 0.0)
    x = x + _L1_gnn_ref(h, adj, L1_gnn_W, L1_gnn_b)
    return x

_drawn_inputs = setup_inputs


def setup_inputs(seed=0):
    import zlib

    import numpy as np

    out = dict(_drawn_inputs(seed))
    spreads = {}
    factors = {'L0_gnn_W1': 5.883, 'L0_gnn_b1': 8.0, 'L1_gnn_b': 5.22}
    for name, (base, spread) in spreads.items():
        noise = np.random.default_rng([zlib.crc32(name.encode()), seed]).standard_normal(out[name].shape)
        drawn = base * np.exp(spread * noise) if base else spread * noise
        out[name] = jnp.asarray(drawn.astype(out[name].dtype))
    for name, factor in factors.items():
        out[name] = (out[name] * factor).astype(out[name].dtype)
    return out
```

```python
from contextlib import ExitStack

import concourse.bass as bass
from concourse import mybir

F32 = mybir.dt.float32
F32R = mybir.dt.float32r
U32 = mybir.dt.uint32
ACT = mybir.ActivationFunctionType
ALU = mybir.AluOpType
AX_X = mybir.AxisListType.X

N = 4096
F = 128
P = 128
QD = 4
R = 32
TILES = N // P
U = 4
GROUPS = TILES // U
GI = U * P
UNIT_COLS = U * R
CHUNK_UNITS = 2
CHUNK_COLS = CHUNK_UNITS * UNIT_COLS
CHUNKS = GROUPS // CHUNK_UNITS
SLOTS = 4
TSLOTS = 4
TOPK = 4
LN_EPS = 1e-5
DMA = 16


def gnn_kernel(nc, x, adj, W1, b1, W2, b2, W, b, out):
    x_v = x.rearrange("(q t s) f -> q s t f", q=QD, t=TILES)
    out_v = out.rearrange("(q g u s) f -> q s g u f", q=QD, g=GROUPS, u=U)
    adj_v = adj.rearrange("(Q g u r) (q c) -> q r g u Q c", Q=QD, g=GROUPS, u=U, q=QD)
    hw_dram = nc.dram_tensor("hw_scratch", (N, F), F32).ap()
    table = nc.dram_tensor("neighbour_table", (N, F), F32).ap()
    hw_v = hw_dram.rearrange("(q g u s) f -> q s g u f", q=QD, g=GROUPS, u=U)
    hw_tv = hw_dram.rearrange("(q t s) f -> q s t f", q=QD, t=TILES)
    table_v = table.rearrange("(q t s) f -> q s t f", q=QD, t=TILES)

    ctx = ExitStack()
    with ctx:
        def sb(name, shape, dt=F32):
            return ctx.enter_context(nc.sbuf_tensor(name, shape, dt))

        def sem(name):
            return ctx.enter_context(nc.semaphore(name))

        araw = sb("araw", [P, SLOTS, U * QD, CHUNK_COLS])
        tr = sb("tr", [P, TSLOTS, U, GI])
        xs = sb("xs", [P, TILES, F])
        hs = sb("hs", [P, TILES, F])
        ys = sb("ys", [P, TILES, F])
        zt_hi = sb("zt_hi", [P, QD, TILES, R], F32R)
        zt_lo = sb("zt_lo", [P, QD, TILES, R], F32R)
        sq_rows = sb("sq_rows", [P, QD, TILES, R], F32R)
        out_t = sb("out_t", [P, GI])
        z_st = sb("z_st", [P, U, F])
        t_st = sb("t_st", [P, U, F])
        zs_hi = sb("zs_hi", [P, 2, P], F32R)
        zs_lo = sb("zs_lo", [P, 2, P], F32R)
        w1s = sb("w1s", [F, F])
        w2s = sb("w2s", [F, F])
        ws_t = sb("ws_t", [F, F])
        wn_t = sb("wn_t", [F, F])
        bias = sb("bias", [P, F])
        ident = sb("ident", [P, P])
        fold = sb("fold", [P, P])
        neghalf = sb("neghalf", [P, P])
        pick = sb("pick", [P, P], F32R)
        part = sb("part", [P, 2, CHUNKS, U * QD])
        deg = sb("deg", [P, TILES])
        dinv = sb("dinv", [P, TILES])
        tmp32 = sb("tmp32", [P, TILES])
        mv = sb("mv", [P, TILES, 2])
        negmr = sb("negmr", [P, TILES])
        nsq = sb("nsq", [P, TILES])
        vals = sb("vals", [P, TILES, TOPK])
        idx = sb("idx", [P, TILES, TOPK], U32)
        m8 = sb("m8", [P, 2, 8])
        i8 = sb("i8", [P, 2, 8], U32)
        idx_st = sb("idx_st", [P, U * TOPK], U32)
        stats4 = sb("stats4", [P, U, 6])

        stats = tr[:, 0, 0, 0:TILES * 6].rearrange("p (t k) -> p t k", k=6)
        w_raw = tr[:, 1, 0, 0:2 * F]
        keys = [araw[:, 2 + i].rearrange("p c k -> p (c k)") for i in range(2)]
        hw_sb = tr[:, 2:4].rearrange("p a b (c f) -> p (a b c) f", f=F)
        gath = zt_lo[:].bitcast(F32).rearrange("p q t s -> p (q t s)")[:, 0:U * TOPK * F]\
            .rearrange("p (u k f) -> p u k f", u=U, k=TOPK)

        ps = ctx.enter_context(nc.psum_tensor("ps", [P, 8, 512], F32))
        acc = [ps[:, 0], ps[:, 1]]
        ps_z = ps[:, 2]
        ps_t = ps[:, 3]
        ps_q = ps[:, 4]
        ps_d = ps[:, 5]
        junk = ps[:, 6]

        x_in = sem("x_in")
        w_in = sem("w_in")
        bias_in = sem("bias_in")
        bias_used = sem("bias_used")
        consts = sem("consts")
        const_st = sem("const_st")
        a_in = [sem(f"a_in{i}") for i in range(SLOTS)]
        a_used = sem("a_used")
        t_ready = sem("t_ready")
        t_used = sem("t_used")
        acc_done = sem("acc_done")
        acc_read = sem("acc_read")
        part_done = sem("part_done")
        deg_mm = sem("deg_mm")
        deg_done = sem("deg_done")
        sqrt_done = sem("sqrt_done")
        y_ready = sem("y_ready")
        var_ready = sem("var_ready")
        ln_ready = sem("ln_ready")
        h_done = sem("h_done")
        ht_mm = sem("ht_mm")
        ht_ev = sem("ht_ev")
        hw_mm = sem("hw_mm")
        hw_ev = sem("hw_ev")
        z_out = [sem("z_out0"), sem("z_out1")]
        hw_in = sem("hw_in")
        wt_mm = sem("wt_mm")
        wt_ev = sem("wt_ev")
        z_mm = sem("z_mm")
        z_done = sem("z_done")
        sq_done = sem("sq_done")
        zt_mm = sem("zt_mm")
        zh_done = sem("zh_done")
        zt_ev = sem("zt_ev")
        zl_done = sem("zl_done")
        q_mm = sem("q_mm")
        qh_done = sem("qh_done")
        q_done = sem("q_done")
        nsq_done = sem("nsq_done")
        zs_ready = sem("zs_ready")
        bank_mm = sem("bank_mm")
        key_ev = sem("key_ev")
        max_done = sem("max_done")
        top_kept = sem("top_kept")
        s_arg = sem("s_arg")
        s_root = sem("s_root")
        s_exp = sem("s_exp")
        deg2 = sem("deg2")
        deg2_root = sem("deg2_root")
        gw_ready = sem("gw_ready")
        table_out = sem("table_out")
        x_again = sem("x_again")
        idx_ready = sem("idx_ready")
        gath_in = sem("gath_in")
        gath_used = sem("gath_used")
        sd_done = sem("sd_done")
        h2_done = sem("h2_done")
        kept = sem("kept")
        xbb_ready = sem("xbb_ready")
        dve = sem("dve")
        pool = sem("pool")

        block = ctx.enter_context(nc.Block())

        first_loads = []
        for g in range(GROUPS):
            own = g // CHUNK_UNITS
            for c in [c for c in range(CHUNKS) if c != own] + [own]:
                units = [w for w in (2 * c, 2 * c + 1) if w <= g]
                first_loads.append((g, c * CHUNK_COLS, CHUNK_COLS, True, units))
        for g in range(GROUPS - 1):
            w = g + 1
            while w < GROUPS:
                n = 1 if w % 2 else 2
                first_loads.append((g, w * UNIT_COLS, n * UNIT_COLS, False, list(range(w, w + n))))
                w += n
        LOADS1 = len(first_loads)
        assert LOADS1 % SLOTS == 0
        UNITS = GROUPS * GROUPS
        PER_PASS = GROUPS * CHUNKS
        ACC1 = 2 * GROUPS - 1
        F1 = [GROUPS - 1] + list(range(GROUPS - 1))

        def load(sp, n, g, c0, cols):
            slot = n % SLOTS
            for q in range(QD):
                dst = araw[R * q:R * q + R, slot, :, 0:cols].rearrange("p (u Q) c -> p u Q c", u=U)
                for u in range(U):
                    sp.dma_start(dst[:, u], adj_v[q, :, g, u, :, c0:c0 + cols]).then_inc(a_in[slot], DMA)

        PER_LOAD = QD * U * DMA
        CONSTS = 1 + QD

        def wait_alone(eng, signal, value):
            if not isinstance(value, int):
                value = eng.to_reg(value)
                eng.wait_ge(x_in, QD * DMA)
            eng.wait_ge(signal, value)

        @block.sync
        def _(sp):
            for q in range(QD):
                sp.dma_start(xs[R * q:R * q + R], x_v[q]).then_inc(x_in, DMA)
            sp.dma_start(w1s[:], W1).then_inc(w_in, DMA)
            sp.dma_start(w2s[:], W2).then_inc(w_in, DMA)
            sp.dma_start(w_raw, W).then_inc(w_in, DMA)
            sp.dma_start(bias[:], b1.partition_broadcast(P)).then_inc(bias_in, DMA)
            for n, (g, c0, cols, _, _) in enumerate(first_loads):
                if n >= SLOTS:
                    sp.wait_ge(a_used, n - SLOTS + 1)
                load(sp, n, g, c0, cols)
            sp.wait_ge(z_mm, GROUPS)
            for q in range(QD):
                sp.dma_start(xs[R * q:R * q + R], x_v[q]).then_inc(x_again, DMA)
            sp.wait_ge(z_done, GROUPS)
            sp.dma_start(bias[:], b2.partition_broadcast(P)).then_inc(bias_in, DMA)
            sp.wait_ge(t_used, UNITS)
            for p in range(2):
                sp.wait_ge(z_out[p], GROUPS // 2 * QD * DMA)
            for q in range(QD):
                sp.dma_start(hw_sb[R * q:R * q + R], hw_tv[q]).then_inc(hw_in, DMA)
            sp.wait_ge(kept, 1)
            sp.dma_start(bias[:], b.partition_broadcast(P)).then_inc(bias_in, DMA)
            for n in range(SLOTS // 2):
                sp.wait_ge(a_used, LOADS1 - SLOTS + 1 + n)
                load(sp, n, 0, n * CHUNK_COLS, CHUNK_COLS)
            sp.wait_ge(max_done, TILES)
            for n in range(SLOTS // 2, SLOTS):
                load(sp, n, 0, n * CHUNK_COLS, CHUNK_COLS)
            sp.wait_ge(gw_ready, 1)
            for q in range(QD):
                sp.dma_start(table_v[q], hw_sb[R * q:R * q + R]).then_inc(table_out, DMA)
            with sp.Fori(1, GROUPS) as g:
                for c in range(CHUNKS):
                    sp.wait_ge(a_used, g * CHUNKS + (LOADS1 + c - SLOTS + 1))
                    load(sp, c, g, c * CHUNK_COLS, CHUNK_COLS)
            with sp.Fori(0, GROUPS) as g:
                for c in range(CHUNKS):
                    sp.wait_ge(a_used, g * CHUNKS + (LOADS1 + PER_PASS + c - SLOTS + 1))
                    load(sp, c, g, c * CHUNK_COLS, CHUNK_COLS)
            for p in range(2):
                sp.wait_ge(z_out[p], GROUPS * QD * DMA)

        @block.gpsimd
        def _(gp):
            gp.wait_ge(const_st, 3)
            gp.affine_select(out=ident[:], in_=ident[:], compare_op=ALU.not_equal, fill=1.0, base=0,
                             pattern=[[-1, P]], channel_multiplier=1).then_inc(consts, 1)
            fold_v = fold[:].rearrange("p (a b) -> p a b", b=R)
            for q in range(QD):
                gp.affine_select(out=fold_v, in_=fold_v, compare_op=ALU.not_equal, fill=1.0, base=-R * q,
                                 pattern=[[0, QD], [-1, R]], channel_multiplier=1).then_inc(consts, 1)
                gp.wait_ge(consts, 2 + q)
            def stage_tile(it, par):
                if not (isinstance(it, int) and it < 2):
                    gp.wait_ge(bank_mm, (it - 1) * 4)
                dst_h = zs_hi[:, par].rearrange("p (q s) -> p q s", s=R)
                dst_l = zs_lo[:, par].rearrange("p (q s) -> p q s", s=R)
                gp.tensor_copy(dst_h, zt_hi[:, :, bass.ds(it, 1), :].rearrange("p q o s -> p q (o s)")).then_inc(zs_ready, 1)
                gp.tensor_copy(dst_l, zt_lo[:, :, bass.ds(it, 1), :].rearrange("p q o s -> p q (o s)")).then_inc(zs_ready, 1)

            def keep_top(it, par):
                gp.wait_ge(max_done, it + 1)
                gp.tensor_copy(vals[:, bass.ds(it, 1), :].rearrange("p o k -> p (o k)"), m8[:, par, 0:TOPK]).then_inc(top_kept, 1)
                gp.tensor_copy(idx[:, bass.ds(it, 1), :].rearrange("p o k -> p (o k)"), i8[:, par, 0:TOPK]).then_inc(top_kept, 1)

            gp.wait_ge(zl_done, GROUPS)
            for par in range(2):
                stage_tile(par, par)
            gp.wait_ge(x_again, QD * DMA)
            gp.wait_ge(bias_in, 2 * DMA)
            gp.tensor_tensor(xs[:], xs[:], bias[:].unsqueeze(1).broadcast_to([P, TILES, F]), ALU.add).then_inc(kept, 1)
            with gp.Fori(1, TILES // 2) as pair:
                for par in range(2):
                    stage_tile(pair * 2 + par, par)
                    keep_top(pair * 2 + (par - 2), par)
            for par in range(2):
                keep_top(TILES - 2 + par, par)
            gp.wait_ge(table_out, QD * DMA)
            gp.wait_ge(top_kept, 2 * TILES)
            def gather_group(g):
                first = isinstance(g, int)
                if not first:
                    gp.wait_ge(gath_used, g)
                    gp.wait_ge(gath_in, g * (U * TOPK * DMA))
                gp.tensor_copy(idx_st[:].rearrange("p (u k) -> p u k", u=U), idx[:, bass.ds(g * U, U), :]).then_inc(idx_ready, 1)
                wait_alone(gp, idx_ready, g + 1)
                for u in range(U):
                    for k in range(TOPK):
                        gp.indirect_dma_start(
                            out=gath[:, u, k, :], out_offset=None, in_=table,
                            in_offset=bass.IndirectOffsetOnAxis(ap=idx_st[:, u * TOPK + k:u * TOPK + k + 1], axis=0),
                            bounds_check=N - 1).then_inc(gath_in, DMA)

            def keep_h2(g):
                gp.wait_ge(h2_done, g + 1)
                gp.tensor_copy(hs[:, bass.ds(g * U, U), :], z_st[:]).then_inc(kept, 1)
            gather_group(0)
            with gp.Fori(1, GROUPS) as g:
                gather_group(g)
                keep_h2(g - 1)
            keep_h2(GROUPS - 1)
            gp.wait_ge(q_done, 2 * GROUPS)
            gp.wait_ge(bias_in, 3 * DMA)
            gp.tensor_tensor(xs[:], xs[:], bias[:].unsqueeze(1).broadcast_to([P, TILES, F]), ALU.add).then_inc(xbb_ready, 1)

        @block.scalar
        def _(act):
            act.wait_ge(var_ready, 1)
            act.activation(tmp32[:], tmp32[:], ACT.Sqrt).then_inc(sqrt_done, 1)
            act.wait_ge(ln_ready, 1)
            for t in range(TILES):
                act.activation(hs[:, t], xs[:, t], ACT.Relu, bias=negmr[:, t:t + 1], scale=tmp32[:, t:t + 1]).then_inc(h_done, 1)
            act.wait_ge(wt_mm, 1)
            act.activation(ws_t[:], ps_z[:, 0:F], ACT.Copy).then_inc(wt_ev, 1)
            act.activation(wn_t[:], ps_z[:, F:2 * F], ACT.Copy).then_inc(wt_ev, 1)
            for g in range(GROUPS):
                act.wait_ge(ht_mm, g + 1)
                act.activation(t_st[:].rearrange("p u f -> p (u f)"), ps_t, ACT.Copy).then_inc(ht_ev, 1)
                act.wait_ge(hw_mm, g + 1)
                if g >= 1:
                    act.wait_ge(z_out[(g - 1) % 2], ((g - 1) // 2 + 1) * QD * DMA)
                act.activation(z_st[:].rearrange("p u f -> p (u f)"), ps_q, ACT.Copy).then_inc(hw_ev, 1)
                act.wait_ge(hw_ev, g + 1)
                for q in range(QD):
                    act.dma_start(hw_v[q, :, g], z_st[R * q:R * q + R]).then_inc(z_out[g % 2], DMA)

            def finish_first(k):
                g = F1[k]
                act.wait_ge(z_done, k + 1)
                if k >= 1:
                    act.wait_ge(sq_done, k)
                for u in range(U):
                    t = g * U + u
                    ins = act.activation(junk[:, u * F:u * F + F], z_st[:, u], ACT.Square, accum_out=nsq[:, t:t + 1])
                ins.then_inc(sq_done, 1)
                act.wait_ge(zt_mm, k + 1)
                act.activation(zt_hi[:, :, g * U:g * U + U, :].rearrange("p q u s -> p u q s"),
                               ps_t.rearrange("p (u q s) -> p u q s", u=U, q=QD), ACT.Copy).then_inc(zh_done, 1)
                if k >= 1:
                    act.wait_ge(q_mm, k)
                act.activation(t_st[:].rearrange("p u f -> p (u f)"), ps_t, ACT.Square).then_inc(zt_ev, 1)
                act.wait_ge(q_mm, k + 1)
                act.activation(sq_rows[0:R, :, g * U:g * U + U, :].rearrange("p q u s -> p u q s"),
                               ps_q[0:R].rearrange("p (u q s) -> p u q s", u=U, q=QD), ACT.Copy).then_inc(qh_done, 1)
                act.activation(z_st[R:2 * R].rearrange("p u f -> p (u f)").bitcast(F32R), ps_q[R:2 * R], ACT.Copy).then_inc(qh_done, 1)

            def root(g):
                act.wait_ge(deg_done, g + 1)
                act.activation(tmp32[:, g * U:g * U + U], deg[:, g * U:g * U + U], ACT.Sqrt).then_inc(sqrt_done, 1)

            for g in range(GROUPS):
                root(g)
                act.wait_ge(acc_done, g + 1)
                dst = xs[:, g * U:g * U + U].rearrange("p u f -> p (u f)") if g < GROUPS - 1 else out_t[:]
                act.activation(dst, acc[g % 2], ACT.Copy).then_inc(acc_read, 1)
            for k in range(GROUPS):
                finish_first(k)
            act.wait_ge(nsq_done, 1)
            def leave(it, par):
                for c in range(4):
                    if c == 0 and not (isinstance(it, int) and it < 2):
                        act.wait_ge(max_done, it - 1)
                    wait_alone(act, bank_mm, it * 4 + (c + 1))
                    act.activation(keys[par][:, c * 1024:c * 1024 + 1024],
                                   ps[:, 2 * c:2 * c + 2].rearrange("p a b -> p (a b)"), ACT.Identity,
                                   bias=nsq[:, bass.ds(it, 1)], scale=2.0).then_inc(key_ev, 1)
            act.wait_ge(a_used, LOADS1)
            for par in range(2):
                leave(par, par)
            with act.Fori(1, TILES // 2) as pair:
                for par in range(2):
                    leave(pair * 2 + par, par)
            vals_f = vals[:].rearrange("p t k -> p (t k)")
            act.wait_ge(s_arg, 1)
            act.activation(vals_f, vals_f, ACT.Sqrt).then_inc(s_root, 1)
            act.wait_ge(s_root, 1)
            act.activation(vals_f, vals_f, ACT.Exp, scale=-0.5).then_inc(s_exp, 1)
            act.wait_ge(deg2, 1)
            act.activation(tmp32[:], tmp32[:], ACT.Sqrt).then_inc(deg2_root, 1)

            def evacuate(n, bank):
                act.wait_ge(acc_done, n + 1)
                act.wait_ge(z_mm, n - ACC1 + GROUPS)
                act.wait_ge(z_done, n - ACC1 + GROUPS)
                act.activation(out_t[:], acc[bank], ACT.Copy).then_inc(acc_read, 1)

            def finish_second(g):
                act.wait_ge(var_ready, g + 2)
                act.activation(tmp32[:, 0:U], tmp32[:, 0:U], ACT.Sqrt).then_inc(sd_done, 1)
                act.wait_ge(kept, g + 1)
                act.wait_ge(zt_mm, g + GROUPS)
                wait_alone(act, z_done, g + (GROUPS + 1))
                for u in range(U):
                    ins = act.activation(z_st[:, u], xs[:, bass.ds(g * U + u, 1), :].rearrange("p o f -> p (o f)"), ACT.Relu,
                                         bias=negmr[:, u:u + 1], scale=tmp32[:, u:u + 1])
                ins.then_inc(h2_done, 1)
                act.wait_ge(zt_mm, g + (GROUPS + 1))
                act.wait_ge(q_mm, g + GROUPS)
                act.activation(t_st[:].rearrange("p u f -> p (u f)"), ps_t, ACT.Copy).then_inc(zt_ev, 1)

            with act.Fori(0, GROUPS // 2) as pair:
                for i in range(2):
                    evacuate(pair * 2 + (ACC1 + i), (ACC1 + i) % 2)
                    finish_second(pair * 2 + i)
            with act.Fori(0, GROUPS // 2) as pair:
                for i in range(2):
                    evacuate(pair * 2 + (ACC1 + GROUPS + i), (ACC1 + i) % 2)
                    g = pair * 2 + i
                    act.wait_ge(z_done, g + (2 * GROUPS + 1))
                    src = (z_st, t_st)[i]
                    for q in range(QD):
                        act.dma_start(out_v[q, :, bass.ds(g, 1), :, :].rearrange("s o u f -> s (o u) f"),
                                      src[R * q:R * q + R]).then_inc(z_out[i], DMA)

        @block.vector
        def _(v):
            count = [0]

            def link(ins):
                count[0] += 1
                ins.then_inc(dve, 1)
                v.wait_ge(dve, count[0])

            v.memset(ident[:], 0.0).then_inc(const_st, 1)
            v.memset(fold[:], 0.0).then_inc(const_st, 1)
            v.memset(neghalf[:], -0.5).then_inc(const_st, 1)
            link(v.memset(pick[:].bitcast(F32), 0.0))
            v.memset(pick[0:1].bitcast(F32), 1.0)
            v.memset(pick[R:R + 1].bitcast(F32), 1.0)
            v.memset(sq_rows[2 * R:P].bitcast(F32), 0.0)
            v.wait_ge(x_in, QD * DMA)
            for t in range(TILES):
                ins = v.bn_stats(out=stats[:, t], in_=xs[:, t])
            link(ins)
            for t in range(TILES):
                ins = v.bn_aggr(out=mv[:, t], in_=stats[:, t])
            link(ins)
            v.tensor_scalar(tmp32[:], mv[:, :, 1], LN_EPS, None, ALU.add).then_inc(var_ready, 1)
            v.wait_ge(sqrt_done, 1)
            link(v.reciprocal(tmp32[:], tmp32[:]))
            v.scalar_tensor_tensor(negmr[:], mv[:, :, 0], -1.0, tmp32[:], ALU.mult, ALU.mult).then_inc(ln_ready, 1)

            def transposed(k, slot, off):
                tr_v = tr[:, k % TSLOTS].rearrange("p t (c s) -> p t c s", s=R)
                src = araw[:, slot, :, off:off + UNIT_COLS].rearrange("p c (t s) -> p t c s", s=R)
                return v.transpose(tr_v, src)

            k = 0
            v.wait_ge(wt_ev, 2)
            for n, (g, c0, cols, sums, units) in enumerate(first_loads):
                if sums and n == g * CHUNKS:
                    deg_chunks = 0
                slot = n % SLOTS
                v.wait_ge(a_in[slot], (n // SLOTS + 1) * PER_LOAD)
                for w in units:
                    if k >= TSLOTS:
                        v.wait_ge(t_used, k - TSLOTS + 1)
                    ins = transposed(k, slot, w * UNIT_COLS - c0)
                    ins.then_inc(t_ready, 1)
                    k += 1
                if sums:
                    if deg_chunks == 0 and g >= 2:
                        v.wait_ge(deg_mm, g - 1)
                    ins = v.tensor_reduce(part[:, g % 2, deg_chunks], araw[:, slot], axis=AX_X, op=ALU.add)
                    deg_chunks += 1
                    ins.then_inc(part_done, 1)
                    v.wait_ge(part_done, n + 1)
                    v.nop().then_inc(a_used, 1)
                else:
                    v.wait_ge(t_ready, k)
                    v.nop().then_inc(a_used, 1)
                if sums and deg_chunks == CHUNKS:
                    v.wait_ge(deg_mm, g + 1)
                    ds_v = ps_d[:, 0:U * QD].rearrange("p (u q) -> p u q", u=U)
                    for q in range(QD):
                        ins = v.tensor_copy(deg[R * q:R * q + R, g * U:g * U + U], ds_v[R * q:R * q + R, :, q])
                    ins.then_inc(deg_done, 1)
                    v.wait_ge(sqrt_done, g + 2)
                    link(v.reciprocal(dinv[:, g * U:g * U + U], tmp32[:, g * U:g * U + U]))
                    v.wait_ge(h_done, TILES)
                    v.tensor_tensor(ys[:, g * U:g * U + U], hs[:, g * U:g * U + U],
                                    dinv[:, g * U:g * U + U].unsqueeze(2).broadcast_to([P, U, F]), ALU.mult).then_inc(y_ready, 1)
                last_of_group = n + 1 == LOADS1 or first_loads[n + 1][0] != g
                done = None
                if not sums and last_of_group:
                    done = g + 1
                elif n + 1 == GROUPS * CHUNKS:
                    done = 0
                if done is not None:
                    kf, gf = done, F1[done]
                    if kf >= 1:
                        v.wait_ge(acc_done, GROUPS + kf)
                        v.wait_ge(z_mm, kf)
                        v.tensor_tensor(out_t[:], acc[(GROUPS + kf - 1) % 2], xs[:, gf * U:gf * U + U].rearrange("p u f -> p (u f)"),
                                        ALU.add).then_inc(acc_read, 1)
                    v.wait_ge(z_mm, kf + 1)
                    if kf >= 1:
                        v.wait_ge(q_done, kf)
                        v.wait_ge(zt_mm, kf)
                        v.wait_ge(sq_done, kf)
                    else:
                        for p in range(2):
                            v.wait_ge(z_out[p], GROUPS // 2 * QD * DMA)
                        v.wait_ge(bias_in, DMA)
                    for u in range(U):
                        t = gf * U + u
                        ins = v.scalar_tensor_tensor(z_st[:, u], ps_z[:, u * F:u * F + F], dinv[:, t:t + 1], bias[:], ALU.mult, ALU.add)
                    link(ins)
                    v.scalar_tensor_tensor(z_st[:], z_st[:], 0.1, z_st[:], ALU.mult, ALU.max).then_inc(z_done, 1)
                    v.wait_ge(zt_ev, kf + 1)
                    v.tensor_tensor(zt_lo[:, :, gf * U:gf * U + U, :].rearrange("p q u s -> p u q s"),
                                    ps_t.rearrange("p (u q s) -> p u q s", u=U, q=QD),
                                    zt_hi[:, :, gf * U:gf * U + U, :].rearrange("p q u s -> p u q s").bitcast(F32),
                                    ALU.subtract).then_inc(zl_done, 1)
                    v.wait_ge(qh_done, 2 * kf + 2)
                    v.tensor_tensor(sq_rows[R:2 * R, :, gf * U:gf * U + U, :].rearrange("p q u s -> p u q s"),
                                    ps_q[R:2 * R].rearrange("p (u q s) -> p u q s", u=U, q=QD),
                                    z_st[R:2 * R].rearrange("p u (q s) -> p u q s", s=R), ALU.subtract).then_inc(q_done, 1)
            v.wait_ge(sq_done, GROUPS)
            v.tensor_scalar(nsq[:], nsq[:], -1.0, None, ALU.mult).then_inc(nsq_done, 1)

            def search(it, par):
                if not (isinstance(it, int) and it < 2):
                    v.wait_ge(top_kept, (it - 1) * 2)
                wait_alone(v, key_ev, it * 4 + 4)
                v.max(m8[:, par], keys[par]).then_inc(dve, 1)
                wait_alone(v, dve, it + (count[0] + 1))
                v.max_index(i8[:, par], m8[:, par], keys[par]).then_inc(max_done, 1)

            for par in range(2):
                search(par, par)
            with v.Fori(1, TILES // 2) as pair:
                for par in range(2):
                    search(pair * 2 + par, par)
            count[0] += TILES
            vals_f = vals[:].rearrange("p t k -> p (t k)")
            v.wait_ge(top_kept, 2 * TILES)
            link(v.tensor_scalar(vals_f, vals_f, -1.0, 0.0, ALU.mult, ALU.max))
            v.tensor_scalar(vals_f, vals_f, 1e-10, None, ALU.add).then_inc(s_arg, 1)
            v.wait_ge(s_exp, 1)
            link(v.tensor_reduce(tmp32[:], vals[:], axis=AX_X, op=ALU.add))
            v.tensor_tensor(tmp32[:], tmp32[:], deg[:], ALU.add).then_inc(deg2, 1)
            v.wait_ge(deg2_root, 1)
            link(v.reciprocal(dinv[:], tmp32[:]))
            for g in range(GROUPS):
                sl = slice(g * U, g * U + U)
                v.tensor_tensor(ys[:, sl], hs[:, sl], dinv[:, sl].unsqueeze(2).broadcast_to([P, U, F]), ALU.mult).then_inc(y_ready, 1)
            v.wait_ge(hw_in, QD * DMA)
            v.tensor_tensor(hw_sb, hw_sb, dinv[:].unsqueeze(2).broadcast_to([P, TILES, F]), ALU.mult).then_inc(gw_ready, 1)

            base2 = count[0]
            PER_FINISH2 = 10

            def finish_second(g):
                v.wait_ge(z_mm, g + (GROUPS + 1))
                v.wait_ge(gath_in, (g + 1) * (U * TOPK * DMA))
                v.wait_ge(kept, 1)
                n = [0]

                def chain(ins):
                    n[0] += 1
                    ins.then_inc(dve, 1)
                    wait_alone(v, dve, g * PER_FINISH2 + (base2 + n[0]))

                for kk in range(TOPK):
                    for u in range(U):
                        s_k = vals[:, bass.ds(g * U + u, 1), kk:kk + 1].rearrange("p o k -> p (o k)")
                        own = out_t[:, u * F:u * F + F]
                        before = ps_z[:, u * F:u * F + F] if kk == 0 else own
                        ins = v.scalar_tensor_tensor(own, gath[:, u, kk], s_k, before, ALU.mult, ALU.add)
                    chain(ins)
                for u in range(U):
                    x_u = xs[:, bass.ds(g * U + u, 1), :].rearrange("p o f -> p (o f)")
                    ins = v.scalar_tensor_tensor(x_u, out_t[:, u * F:u * F + F], dinv[:, bass.ds(g * U + u, 1)], x_u, ALU.mult, ALU.add)
                chain(ins)
                for u in range(U):
                    ins = v.bn_stats(out=stats4[:, u], in_=xs[:, bass.ds(g * U + u, 1), :].rearrange("p o f -> p (o f)"))
                chain(ins)
                v.nop().then_inc(gath_used, 1)
                for u in range(U):
                    ins = v.bn_aggr(out=mv[:, u], in_=stats4[:, u])
                chain(ins)
                v.wait_ge(zt_ev, g + GROUPS)
                v.tensor_scalar(tmp32[:, 0:U], mv[:, 0:U, 1], LN_EPS, None, ALU.add).then_inc(var_ready, 1)
                v.wait_ge(sd_done, g + 1)
                chain(v.reciprocal(tmp32[:, 0:U], tmp32[:, 0:U]))
                chain(v.scalar_tensor_tensor(negmr[:, 0:U], mv[:, 0:U, 0], -1.0, tmp32[:, 0:U], ALU.mult, ALU.mult))
                v.nop().then_inc(z_done, 1)
                v.wait_ge(q_mm, g + (GROUPS + 1))
                x_g = xs[:, bass.ds(g * U, U), :]
                chain(v.tensor_tensor(x_g, ps_q.rearrange("p (u f) -> p u f", u=U), x_g, ALU.add))
                v.nop().then_inc(q_done, 1)
                assert n[0] == PER_FINISH2

            def product(g, base_load, base_unit):
                for c in range(CHUNKS):
                    v.wait_ge(a_in[c], (g + (base_load // SLOTS + 1)) * PER_LOAD)
                    for j in range(CHUNK_UNITS):
                        w = c * CHUNK_UNITS + j
                        v.wait_ge(t_used, g * GROUPS + (base_unit + w - TSLOTS + 1))
                        transposed(w, c, j * UNIT_COLS).then_inc(t_ready, 1)
                    v.wait_ge(t_ready, g * GROUPS + (base_unit + w + 1))
                    v.nop().then_inc(a_used, 1)

            v.wait_ge(table_out, QD * DMA)
            with v.Fori(0, GROUPS) as g:
                product(g, LOADS1, UNITS)
                finish_second(g)
            with v.Fori(0, GROUPS // 2) as pair:
                for i in range(2):
                    g = pair * 2 + i
                    product(g, LOADS1 + PER_PASS, 2 * UNITS)
                    v.wait_ge(z_mm, g + (2 * GROUPS + 1))
                    v.wait_ge(xbb_ready, 1)
                    v.wait_ge(z_out[i], pair * (QD * DMA) + GROUPS // 2 * QD * DMA)
                    v.tensor_tensor((z_st, t_st)[i][:], ps_z.rearrange("p (u f) -> p u f", u=U), xs[:, bass.ds(g * U, U), :],
                                    ALU.add).then_inc(z_done, 1)

        @block.tensor
        def _(pe):
            pe.wait_ge(consts, CONSTS)
            pe.wait_ge(w_in, 3 * DMA)
            pe.transpose(ps_z[:, 0:F], w_raw[:, 0:F], ident[:])
            pe.transpose(ps_z[:, F:2 * F], w_raw[:, F:2 * F], ident[:]).then_inc(wt_mm, 1)

            def four(dst, lhs, rhs):
                for u in range(U):
                    ins = pe.matmul(dst[:, u * F:u * F + F], lhs[:, u * P:u * P + P], rhs, start=True, stop=True)
                return ins

            def transposes(dst, src):
                for u in range(U):
                    ins = pe.transpose(dst[:, u * F:u * F + F], src[:, u], ident[:])
                return ins

            t_flat = t_st[:].rearrange("p u f -> p (u f)")
            for g in range(GROUPS):
                pe.wait_ge(h_done, (g + 1) * U)
                if g >= 1:
                    pe.wait_ge(ht_ev, g)
                transposes(ps_t, hs[:, g * U:g * U + U]).then_inc(ht_mm, 1)
                pe.wait_ge(ht_ev, g + 1)
                if g >= 1:
                    pe.wait_ge(hw_ev, g)
                four(ps_q, t_flat, w2s[:]).then_inc(hw_mm, 1)

            def unit(k, w, ysrc, bank, start, stop):
                for i in range(U):
                    ins = pe.matmul(acc[bank], ysrc[:, w * U + i], tr[:, w_slot(k), i],
                                    start=start and i == 0, stop=stop and i == U - 1)
                ins.then_inc(t_used, 1)
                return ins

            def w_slot(k):
                return k % TSLOTS

            def finish_first(k):
                pe.wait_ge(acc_read, GROUPS + k)
                four(ps_z, out_t[:], w1s[:]).then_inc(z_mm, 1)
                pe.wait_ge(z_done, k + 1)
                if k >= 1:
                    pe.wait_ge(zl_done, k)
                    pe.wait_ge(zt_ev, k)
                transposes(ps_t, z_st[:]).then_inc(zt_mm, 1)
                pe.wait_ge(zt_ev, k + 1)
                if k >= 1:
                    pe.wait_ge(q_done, k)
                pe.matmul(ps_q, neghalf[:], t_flat, start=True, stop=True).then_inc(q_mm, 1)

            k = 0
            group = 0
            order = []
            for n, (g, c0, cols, sums, units) in enumerate(first_loads):
                last = n + 1 == LOADS1 or first_loads[n + 1][0] != g
                order.append((g, sums, units, last))
            opened = False
            for g, sums, units, last in order:
                if sums and last:
                    pe.wait_ge(part_done, (g + 1) * CHUNKS)
                    if g >= 1:
                        pe.wait_ge(deg_done, g)
                    for c in range(CHUNKS):
                        ins = pe.matmul(ps_d[:, 0:U * QD], fold[:], part[:, g % 2, c], start=c == 0, stop=c == CHUNKS - 1)
                    ins.then_inc(deg_mm, 1)
                for w in units:
                    if not opened and group >= 2:
                        pe.wait_ge(acc_read, group - 1)
                    if sums and w == g:
                        pe.wait_ge(y_ready, g + 1)
                    pe.wait_ge(t_ready, k + 1)
                    end = last and w == units[-1]
                    ins = unit(k, w, ys, group % 2, not opened, end)
                    opened = True
                    k += 1
                if last:
                    pe.wait_ge(t_used, k)
                    pe.nop().then_inc(acc_done, 1)
                    group += 1
                    opened = False
                    if group >= GROUPS:
                        finish_first(group - GROUPS)

            def distances(it, par):
                pe.wait_ge(zs_ready, it * 2 + 2)
                for c in range(8):
                    cols = slice(c * 512, c * 512 + 512)
                    if c % 2 == 0 and not (isinstance(it, int) and it < 1):
                        pe.wait_ge(key_ev, it * 4 + (c // 2 - 3))
                    zh = zt_hi[:].rearrange("p q t s -> p (q t s)")[:, cols]
                    zl = zt_lo[:].rearrange("p q t s -> p (q t s)")[:, cols]
                    sq = sq_rows[:].rearrange("p q t s -> p (q t s)")[:, cols]
                    pe.matmul(ps[:, c], pick[:], sq, start=True, stop=False)
                    pe.matmul(ps[:, c], zs_hi[:, par], zl, start=False, stop=False)
                    pe.matmul(ps[:, c], zs_lo[:, par], zh, start=False, stop=False)
                    ins = pe.matmul(ps[:, c], zs_hi[:, par], zh, start=False, stop=True)
                    if c % 2:
                        ins.then_inc(bank_mm, 1)

            pe.wait_ge(q_done, GROUPS)
            for par in range(2):
                distances(par, par)
            with pe.Fori(1, TILES // 2) as pair:
                for par in range(2):
                    distances(pair * 2 + par, par)

            def product(g, n, bank, base_unit, src):
                pe.wait_ge(acc_read, n - 1)
                for w in range(GROUPS):
                    pe.wait_ge(t_ready, g * GROUPS + (base_unit + w + 1))
                    ins = unit(w, w, src, bank, w == 0, w == GROUPS - 1)
                pe.wait_ge(t_used, g * GROUPS + (base_unit + GROUPS))
                pe.nop().then_inc(acc_done, 1)

            pe.wait_ge(y_ready, 2 * GROUPS)
            pe.wait_ge(key_ev, 4 * TILES)
            with pe.Fori(0, GROUPS // 2) as pair:
                for i in range(2):
                    g = pair * 2 + i
                    product(g, g + ACC1, (ACC1 + i) % 2, UNITS, ys)
                    pe.wait_ge(acc_read, g + (ACC1 + 1))
                    pe.wait_ge(z_done, g + GROUPS)
                    four(ps_z, out_t[:], w2s[:]).then_inc(z_mm, 1)
                    pe.wait_ge(h2_done, g + 1)
                    pe.wait_ge(zt_ev, g + GROUPS)
                    transposes(ps_t, z_st[:]).then_inc(zt_mm, 1)
                    pe.wait_ge(zt_ev, g + (GROUPS + 1))
                    pe.wait_ge(q_done, g + GROUPS)
                    four(ps_q, t_flat, ws_t[:]).then_inc(q_mm, 1)
            pe.wait_ge(kept, GROUPS + 1)
            with pe.Fori(0, GROUPS // 2) as pair:
                for i in range(2):
                    g = pair * 2 + i
                    product(g, g + (ACC1 + GROUPS), (ACC1 + i) % 2, 2 * UNITS, hs)
                    pe.wait_ge(acc_read, g + (ACC1 + GROUPS + 1))
                    pe.wait_ge(z_done, g + 2 * GROUPS)
                    four(ps_z, out_t[:], wn_t[:]).then_inc(z_mm, 1)


_INS = ['x', 'adj', 'L0_gnn_W1', 'L0_gnn_b1', 'L0_gnn_W2', 'L0_gnn_b2', 'L1_gnn_W', 'L1_gnn_b']
_OUTS = [((N, F), 'float32')]


def kernel(**inputs):
    import numpy as _np
    import concourse.bacc as _bacc
    from concourse import mybir as _mybir
    from concourse.bass_utils import run_bass_kernel_spmd as _run

    nc = _bacc.Bacc("TRN2", target_bir_lowering=False, num_devices=1)
    arrays, args = {}, []
    for name in _INS:
        a = _np.ascontiguousarray(inputs[name])
        arrays[f"in_{name}_dram"] = a
        args.append(nc.dram_tensor(f"in_{name}_dram", a.shape, _mybir.dt.from_np(a.dtype), kind="ExternalInput").ap())
    for i, (shape, dtype) in enumerate(_OUTS):
        args.append(nc.dram_tensor(f"out_{i}_dram", shape, _mybir.dt.from_np(_np.dtype(dtype)), kind="ExternalOutput").ap())
    gnn_kernel(nc, *args)
    r = _run(nc, [arrays], core_ids=[0])
    return r.results[0]["out_0_dram"]
```

```python
from contextlib import ExitStack

import concourse.bass as bass
from concourse import mybir

F32 = mybir.dt.float32
F32R = mybir.dt.float32r
U32 = mybir.dt.uint32
ACT = mybir.ActivationFunctionType
ALU = mybir.AluOpType
AX_X = mybir.AxisListType.X

N = 4096
F = 128
P = 128
QD = 4
R = 32
TILES = N // P
U = 4
GROUPS = TILES // U
GI = U * P
UNIT_COLS = U * R
CHUNK_UNITS = 2
CHUNK_COLS = CHUNK_UNITS * UNIT_COLS
CHUNKS = GROUPS // CHUNK_UNITS
SLOTS = 4
TSLOTS = 4
TOPK = 4
LN_EPS = 1e-5
DMA = 16


def gnn_kernel(nc, x, adj, W1, b1, W2, b2, W, b, out):
    x_v = x.rearrange("(q t s) f -> q s t f", q=QD, t=TILES)
    out_v = out.rearrange("(q u g s) f -> q s g u f", q=QD, g=GROUPS, u=U)
    adj_v = adj.rearrange("(m g r) (q c) -> q r g m c", m=QD * U, g=GROUPS, q=QD)
    hw_dram = nc.dram_tensor("hw_scratch", (N, F), F32).ap()
    table = nc.dram_tensor("neighbour_table", (N, F), F32).ap()
    hw_v = hw_dram.rearrange("(q u g s) f -> q s g u f", q=QD, g=GROUPS, u=U)
    hw_tv = hw_dram.rearrange("(q t s) f -> q s t f", q=QD, t=TILES)
    table_v = table.rearrange("(q t s) f -> q s t f", q=QD, t=TILES)

    ctx = ExitStack()
    with ctx:
        def sb(name, shape, dt=F32):
            return ctx.enter_context(nc.sbuf_tensor(name, shape, dt))

        def sem(name):
            return ctx.enter_context(nc.semaphore(name))

        araw = sb("araw", [P, SLOTS, U * QD, CHUNK_COLS])
        tr = sb("tr", [P, TSLOTS, U, GI])
        xs = sb("xs", [P, TILES, F])
        hs = sb("hs", [P, TILES, F])
        ys = sb("ys", [P, TILES, F])
        zt_hi = sb("zt_hi", [P, QD, TILES, R], F32R)
        zt_lo = sb("zt_lo", [P, QD, TILES, R], F32R)
        sq_rows = sb("sq_rows", [P, QD, TILES, R], F32R)
        out_t = sb("out_t", [P, GI])
        z_st = sb("z_st", [P, U, F])
        t_st = sb("t_st", [P, U, F])
        zs_hi = sb("zs_hi", [P, 2, P], F32R)
        zs_lo = sb("zs_lo", [P, 2, P], F32R)
        w1s = sb("w1s", [F, F])
        w2s = sb("w2s", [F, F])
        ws_t = sb("ws_t", [F, F])
        wn_t = sb("wn_t", [F, F])
        bias = sb("bias", [P, F])
        ident = sb("ident", [P, P])
        fold = sb("fold", [P, P])
        neghalf = sb("neghalf", [P, P])
        pick = sb("pick", [P, P], F32R)
        part = sb("part", [P, 2, CHUNKS, U * QD])
        deg = sb("deg", [P, TILES])
        dinv = sb("dinv", [P, TILES])
        tmp32 = sb("tmp32", [P, TILES])
        mv = sb("mv", [P, TILES, 2])
        negmr = sb("negmr", [P, TILES])
        nsq = sb("nsq", [P, TILES])
        vals = sb("vals", [P, TILES, TOPK])
        idx = sb("idx", [P, TILES, TOPK], U32)
        m8 = sb("m8", [P, 2, 8])
        i8 = sb("i8", [P, 2, 8], U32)
        idx_st = sb("idx_st", [P, 2, U * TOPK], U32)
        stats4 = sb("stats4", [P, U, 6])

        xs_g = xs[:].rearrange("p (u g) f -> p g u f", g=GROUPS)
        hs_g = hs[:].rearrange("p (u g) f -> p g u f", g=GROUPS)
        ys_g = ys[:].rearrange("p (u g) f -> p g u f", g=GROUPS)
        deg_g = deg[:].rearrange("p (u g) -> p g u", g=GROUPS)
        dinv_g = dinv[:].rearrange("p (u g) -> p g u", g=GROUPS)
        idx_g = idx[:].rearrange("p (u g) k -> p g u k", g=GROUPS)
        zt_hi_g = zt_hi[:].rearrange("p q (u g) s -> p g u q s", g=GROUPS)
        zt_lo_g = zt_lo[:].rearrange("p q (u g) s -> p g u q s", g=GROUPS)
        sq_rows_g = sq_rows[:].rearrange("p q (u g) s -> p g u q s", g=GROUPS)
        out_t_m = out_t[:].rearrange("p (u Q r) -> p Q u r", u=U, Q=QD)

        def by_block(flat):
            return flat.rearrange("p (Q u r) -> p Q u r", Q=QD, u=U)

        stats = out_t[:, 2 * F:2 * F + TILES * 6].rearrange("p (t k) -> p t k", k=6)
        w_raw = out_t[:, 0:2 * F]
        keys = [araw[:, 2 + i].rearrange("p c k -> p (c k)") for i in range(2)]
        hw_sb = tr[:, 2:4].rearrange("p a b (c f) -> p (a b c) f", f=F)
        gath = zt_lo[:].bitcast(F32).rearrange("p q t s -> p (q t s)")\
            .rearrange("p (i u k f) -> p i u k f", i=2, u=U, k=TOPK)

        ps = ctx.enter_context(nc.psum_tensor("ps", [P, 8, 512], F32))
        acc = [ps[:, 0], ps[:, 1]]
        ps_z = ps[:, 2]
        ps_t = ps[:, 3]
        ps_q = ps[:, 4]
        ps_d = ps[:, 5]
        junk = [ps[:, 6], ps[:, 7]]

        x_in = sem("x_in")
        w_in = sem("w_in")
        bias_in = sem("bias_in")
        bias_used = sem("bias_used")
        consts = sem("consts")
        const_st = sem("const_st")
        a_in = [sem(f"a_in{i}") for i in range(SLOTS)]
        t_ready = sem("t_ready")
        t_used = sem("t_used")
        diag_ready = sem("diag_ready")
        diag_used = sem("diag_used")
        part_dve = sem("part_dve")
        part_act = sem("part_act")
        acc_read = sem("acc_read")
        deg_mm = sem("deg_mm")
        deg_done = sem("deg_done")
        sqrt_done = sem("sqrt_done")
        y_ready = sem("y_ready")
        var_ready = sem("var_ready")
        ln_ready = sem("ln_ready")
        h_done = sem("h_done")
        ht_mm = sem("ht_mm")
        ht_ev = sem("ht_ev")
        hw_mm = sem("hw_mm")
        hw_ev = sem("hw_ev")
        z_out = [sem("z_out0"), sem("z_out1")]
        hw_in = sem("hw_in")
        wt_mm = sem("wt_mm")
        wt_ev = sem("wt_ev")
        z_mm = sem("z_mm")
        z_done = sem("z_done")
        sq_done = sem("sq_done")
        zt_mm = sem("zt_mm")
        zt_ev = sem("zt_ev")
        zl_done = sem("zl_done")
        q_mm = sem("q_mm")
        qh_done = sem("qh_done")
        q_done = sem("q_done")
        nsq_done = sem("nsq_done")
        zs_ready = sem("zs_ready")
        bank_mm = sem("bank_mm")
        key_ev = sem("key_ev")
        max_done = sem("max_done")
        top_kept = sem("top_kept")
        s_arg = sem("s_arg")
        s_root = sem("s_root")
        s_exp = sem("s_exp")
        deg2 = sem("deg2")
        deg2_root = sem("deg2_root")
        gw_ready = sem("gw_ready")
        table_out = sem("table_out")
        x_again = sem("x_again")
        idx_ready = sem("idx_ready")
        gath_in = [sem("gath_in0"), sem("gath_in1")]
        gath_used = sem("gath_used")
        x1_done = sem("x1_done")
        stats_done = sem("stats_done")
        aggr_done = sem("aggr_done")
        rsd_done = sem("rsd_done")
        gw_kept = sem("gw_kept")
        sd_done = sem("sd_done")
        h2_done = sem("h2_done")
        kept = sem("kept")
        xb_ready = sem("xb_ready")
        dve = sem("dve")
        pool = sem("pool")

        block = ctx.enter_context(nc.Block())

        part_a = []
        for g in range(GROUPS):
            for c in range(CHUNKS):
                part_a.append((g, c, [(i, min(U, g - i)) for i in range(0, g, U)]))
        part_b = []
        for g in reversed(range(GROUPS - 1)):
            for c in range(CHUNKS):
                part_b.append((g, c, [(i, min(U, GROUPS - i)) for i in range(g + 1, GROUPS, U)]))
        LOADS_A, LOADS1 = len(part_a), len(part_a) + len(part_b)
        assert LOADS1 % SLOTS == 0
        UNITS1 = sum(len(p) for _, _, p in part_a + part_b)
        UNITS = GROUPS * GROUPS
        RING1 = TSLOTS - 1
        F1 = [GROUPS - 1] + list(reversed(range(GROUPS - 1)))
        PER_LOAD = QD * DMA
        EVENS_FIRST = list(range(0, GROUPS, 2)) + list(range(1, GROUPS, 2))
        GATHER = U * TOPK * DMA
        CONSTS = 1 + QD

        def act_sums(g, c):
            return c != CHUNKS - 1 and (c != 1 or g >= 5)

        consumed = []
        k = n_dve = n_act = n_diag = 0
        for g, c, pieces in part_a:
            k += len(pieces)
            n_diag += 1
            n_act += act_sums(g, c)
            n_dve += not act_sums(g, c)
            consumed.append((k, n_diag, n_dve, n_act))
        for g, c, pieces in part_b:
            k += len(pieces)
            consumed.append((k, n_diag, n_dve, n_act))
        units_after = [c[0] for c in consumed]

        def stages_first(n_units):
            return dict(sum_=0, a=1, a2=3, b=4, b2=5, c=6, c2=7) if n_units == 8 else \
                dict(sum_=0, a=1, a2=2, b=2, b2=3, c=3, c2=3)

        def wait_alone(eng, signal, value):
            if not isinstance(value, int):
                value = eng.to_reg(value)
                eng.wait_ge(x_in, QD * DMA)
            eng.wait_ge(signal, value)

        def load(sp, slot, g, c0, cols):
            for q in range(QD):
                if isinstance(g, int):
                    src = adj_v[q, :, g, :, c0:c0 + cols]
                else:
                    src = adj_v[q, :, bass.ds(g, 1), :, c0:c0 + cols].rearrange("r o m c -> r (o m) c")
                sp.dma_start(araw[R * q:R * q + R, slot, :, 0:cols], src).then_inc(a_in[slot], DMA)

        def flat(x3):
            return x3.rearrange("p u f -> p (u f)")

        @block.sync
        def _(sp):
            for q in range(QD):
                sp.dma_start(xs[R * q:R * q + R], x_v[q]).then_inc(x_in, DMA)
            sp.dma_start(w_raw, W).then_inc(w_in, DMA)
            sp.dma_start(w2s[:], W2).then_inc(w_in, DMA)
            sp.dma_start(w1s[:], W1).then_inc(w_in, DMA)
            sp.dma_start(bias[:], b1.partition_broadcast(P)).then_inc(bias_in, DMA)
            for n, (g, c, pieces) in enumerate(part_a + part_b):
                if n >= SLOTS:
                    was = consumed[n - SLOTS]
                    if was[0]:
                        sp.wait_ge(t_ready, was[0])
                    if n - SLOTS < LOADS_A:
                        sp.wait_ge(diag_ready, was[1])
                        if act_sums(part_a[n - SLOTS][0], part_a[n - SLOTS][1]):
                            sp.wait_ge(part_act, was[3])
                        else:
                            sp.wait_ge(part_dve, was[2])
                if n < LOADS_A:
                    load(sp, n % SLOTS, g, c * CHUNK_COLS, CHUNK_COLS)
                else:
                    load(sp, n % SLOTS, g, c * CHUNK_COLS + (g + 1) * R, (GROUPS - 1 - g) * R)
            sp.wait_ge(acc_read, 2 * GROUPS - 1)
            for q in range(QD):
                sp.dma_start(xs[R * q:R * q + R], x_v[q]).then_inc(x_again, DMA)
            sp.wait_ge(z_done, GROUPS)
            sp.dma_start(bias[:], b2.partition_broadcast(P)).then_inc(bias_in, DMA)
            sp.wait_ge(t_used, UNITS1)
            for p in range(2):
                sp.wait_ge(z_out[p], GROUPS // 2 * QD * DMA)
            for q in range(QD):
                sp.dma_start(hw_sb[R * q:R * q + R], hw_tv[q]).then_inc(hw_in, DMA)
            sp.wait_ge(kept, 1)
            sp.dma_start(bias[:], b.partition_broadcast(P)).then_inc(bias_in, DMA)
            for n in range(SLOTS // 2):
                load(sp, n, 0, n * CHUNK_COLS, CHUNK_COLS)
            sp.wait_ge(max_done, TILES)
            for n in range(SLOTS // 2, SLOTS):
                load(sp, n, 0, n * CHUNK_COLS, CHUNK_COLS)
            sp.wait_ge(gw_ready, 1)
            for q in range(QD):
                sp.dma_start(table_v[q], hs[R * q:R * q + R]).then_inc(table_out, DMA)
            def load_group(g2):
                g = g2 % GROUPS if isinstance(g2, int) else sp.snap(g2 % GROUPS)
                for c in range(CHUNKS):
                    taken = CHUNKS + c + 1 if isinstance(g2, int) else (c + 1) * CHUNK_UNITS
                    sp.wait_ge(t_ready, g2 * GROUPS + (UNITS1 + taken - GROUPS))
                    load(sp, c, g, c * CHUNK_COLS, CHUNK_COLS)

            with sp.Fori(1, GROUPS + 1) as g2:
                load_group(g2)
            load_group(GROUPS + 1)
            with sp.Fori(GROUPS + 2, 2 * GROUPS) as g2:
                load_group(g2)
            for p in range(2):
                sp.wait_ge(z_out[p], GROUPS * QD * DMA)

        @block.gpsimd
        def _(gp):
            gp.wait_ge(const_st, 3)
            gp.affine_select(out=ident[:], in_=ident[:], compare_op=ALU.not_equal, fill=1.0, base=0,
                             pattern=[[-1, P]], channel_multiplier=1).then_inc(consts, 1)
            fold_v = fold[:].rearrange("p (a b) -> p a b", b=R)
            for q in range(QD):
                gp.affine_select(out=fold_v, in_=fold_v, compare_op=ALU.not_equal, fill=1.0, base=-R * q,
                                 pattern=[[0, QD], [-1, R]], channel_multiplier=1).then_inc(consts, 1)
                gp.wait_ge(consts, 2 + q)

            def stage_tile(it, par):
                if not (isinstance(it, int) and it < 2):
                    gp.wait_ge(bank_mm, (it - 1) * 4)
                dst_h = zs_hi[:, par].rearrange("p (q s) -> p q s", s=R)
                dst_l = zs_lo[:, par].rearrange("p (q s) -> p q s", s=R)
                gp.tensor_copy(dst_h, zt_hi[:, :, bass.ds(it, 1), :].rearrange("p q o s -> p q (o s)")).then_inc(zs_ready, 1)
                gp.tensor_copy(dst_l, zt_lo[:, :, bass.ds(it, 1), :].rearrange("p q o s -> p q (o s)")).then_inc(zs_ready, 1)

            def keep_top(it, par):
                gp.wait_ge(max_done, it + 1)
                gp.tensor_copy(vals[:, bass.ds(it, 1), :].rearrange("p o k -> p (o k)"), m8[:, par, 0:TOPK]).then_inc(top_kept, 1)
                gp.tensor_copy(idx[:, bass.ds(it, 1), :].rearrange("p o k -> p (o k)"), i8[:, par, 0:TOPK]).then_inc(top_kept, 1)

            gp.wait_ge(zl_done, GROUPS)
            for par in range(2):
                stage_tile(par, par)
            gp.wait_ge(x_again, QD * DMA)
            gp.wait_ge(bias_in, 2 * DMA)
            gp.tensor_tensor(xs[:], xs[:], bias[:].unsqueeze(1).broadcast_to([P, TILES, F]), ALU.add).then_inc(kept, 1)
            with gp.Fori(1, TILES // 2) as pair:
                for par in range(2):
                    stage_tile(pair * 2 + par, par)
                    keep_top(pair * 2 + (par - 2), par)
            for par in range(2):
                keep_top(TILES - 2 + par, par)

            def gather_group(g, i):
                if not isinstance(g, int):
                    gp.wait_ge(gath_used, g - 1)
                    gp.wait_ge(gath_in[i], (g - i) * (GATHER // 2))
                src = idx_g[:, g] if isinstance(g, int) else idx_g[:, bass.ds(g, 1)].rearrange("p o u k -> p (o u) k")
                gp.tensor_copy(idx_st[:, i].rearrange("p (u k) -> p u k", u=U), src).then_inc(idx_ready, 1)
                wait_alone(gp, idx_ready, g + 1)
                for u in range(U):
                    for k in range(TOPK):
                        gp.indirect_dma_start(
                            out=gath[:, i, u, k, :], out_offset=None, in_=table,
                            in_offset=bass.IndirectOffsetOnAxis(ap=idx_st[:, i, u * TOPK + k:u * TOPK + k + 1], axis=0),
                            bounds_check=N - 1).then_inc(gath_in[i], DMA)

            def keep_h2(g):
                gp.wait_ge(h2_done, g + 1)
                dst = hs_g[:, g] if isinstance(g, int) else hs_g[:, bass.ds(g, 1)].rearrange("p o u f -> p (o u) f")
                gp.tensor_copy(dst, z_st[:]).then_inc(kept, 1)
                x_g = xs_g[:, g] if isinstance(g, int) else xs_g[:, bass.ds(g, 1)].rearrange("p o u f -> p (o u) f")
                gp.tensor_tensor(x_g, x_g, bias[:].unsqueeze(1).broadcast_to([P, U, F]), ALU.add).then_inc(xb_ready, 1)

            gp.wait_ge(table_out, QD * DMA)
            gp.wait_ge(top_kept, 2 * TILES)
            for i in range(2):
                gather_group(i, i)
            gp.wait_ge(bias_in, 3 * DMA)
            with gp.Fori(1, GROUPS // 2) as pair:
                for i in range(2):
                    keep_h2(pair * 2 + (i - 2))
                    gather_group(pair * 2 + i, i)
            for i in range(2):
                keep_h2(GROUPS - 2 + i)

        @block.scalar
        def _(act):
            act.wait_ge(var_ready, 1)
            act.activation(tmp32[:], tmp32[:], ACT.Sqrt).then_inc(sqrt_done, 1)
            act.wait_ge(ln_ready, 1)

            def normalize(g):
                for u in range(U):
                    t = GROUPS * u + g
                    act.activation(hs[:, t], xs[:, t], ACT.Relu, bias=negmr[:, t:t + 1], scale=tmp32[:, t:t + 1]).then_inc(h_done, 1)

            for g in range(GROUPS):
                normalize(g)
            act.wait_ge(wt_mm, 1)
            act.activation(ws_t[:], ps_z[:, 0:F], ACT.Copy).then_inc(wt_ev, 1)
            act.activation(wn_t[:], ps_z[:, F:2 * F], ACT.Copy).then_inc(wt_ev, 1)

            n_sums = 0

            def row_sums(g, c):
                nonlocal n_sums
                act.wait_ge(a_in[c], (g + 1) * PER_LOAD)
                if g >= 2:
                    act.wait_ge(deg_mm, g - 1)
                for m in range(QD * U):
                    if n_sums + m >= U:
                        act.wait_ge(pool, n_sums + m - U + 1)
                    act.activation(junk[(m // 2) % 2][:, m % 2 * CHUNK_COLS:(m % 2 + 1) * CHUNK_COLS], araw[:, c, m], ACT.Copy,
                                   accum_out=part[:, g % 2, c, m:m + 1]).then_inc(pool, 1)
                n_sums += QD * U
                act.wait_ge(pool, n_sums)
                act.nop().then_inc(part_act, 1)

            def ht_copy(g):
                act.wait_ge(ht_mm, g + 1)
                if g >= 1:
                    act.wait_ge(hw_mm, g)
                act.activation(flat(t_st[:]), ps_t, ACT.Copy).then_inc(ht_ev, 1)

            def hw_store(g):
                act.wait_ge(hw_mm, g + 1)
                if g >= 1:
                    act.wait_ge(z_out[(g - 1) % 2], ((g - 1) // 2 + 1) * QD * DMA)
                act.activation(flat(z_st[:]), ps_q, ACT.Copy).then_inc(hw_ev, 1)
                act.wait_ge(hw_ev, g + 1)
                for q in range(QD):
                    act.dma_start(hw_v[q, :, g], z_st[R * q:R * q + R]).then_inc(z_out[g % 2], DMA)

            def root(g):
                act.wait_ge(deg_done, g + 1)
                act.activation(tmp32[:, 0:U], deg_g[:, g], ACT.Sqrt).then_inc(sqrt_done, 1)

            def keep_partial(g):
                act.wait_ge(diag_used, g + 1)
                if g < GROUPS - 1:
                    act.activation(xs_g[:, g], acc[g % 2].rearrange("p (u f) -> p u f", u=U), ACT.Copy).then_inc(acc_read, 1)
                else:
                    act.activation(out_t_m, by_block(acc[g % 2]), ACT.Copy).then_inc(acc_read, 1)

            for g in range(GROUPS):
                row_sums(g, 0)
                if g >= 1:
                    keep_partial(g - 1)
                ht_copy(g)
                if act_sums(g, 1):
                    row_sums(g, 1)
                row_sums(g, 2)
                hw_store(g)
                root(g)
            keep_partial(GROUPS - 1)

            def finish_first(k):
                g = F1[k]
                act.wait_ge(z_done, k + 1)
                if k >= 1:
                    act.wait_ge(sq_done, k)
                for u in range(U):
                    t = GROUPS * u + g
                    ins = act.activation(junk[0][:, u * F:u * F + F], z_st[:, u], ACT.Square, accum_out=nsq[:, t:t + 1])
                ins.then_inc(sq_done, 1)
                act.wait_ge(zt_mm, k + 1)
                act.activation(zt_hi_g[:, g], ps_t.rearrange("p (u q s) -> p u q s", u=U, q=QD), ACT.Copy)
                if k >= 1:
                    act.wait_ge(q_mm, k)
                act.activation(flat(t_st[:]), ps_t, ACT.Square).then_inc(zt_ev, 1)
                act.wait_ge(q_mm, k + 1)
                act.activation(sq_rows_g[0:R, g], ps_q[0:R].rearrange("p (u q s) -> p u q s", u=U, q=QD), ACT.Copy).then_inc(qh_done, 1)
                act.activation(flat(z_st[R:2 * R]).bitcast(F32R), ps_q[R:2 * R], ACT.Copy).then_inc(qh_done, 1)

            for k in range(GROUPS):
                finish_first(k)
            act.wait_ge(nsq_done, 1)

            def leave(it, par):
                for c in range(4):
                    if c == 0 and not (isinstance(it, int) and it < 2):
                        act.wait_ge(max_done, it - 1)
                    wait_alone(act, bank_mm, it * 4 + (c + 1))
                    act.activation(keys[par][:, c * 1024:c * 1024 + 1024],
                                   ps[:, 2 * c:2 * c + 2].rearrange("p a b -> p (a b)"), ACT.Identity,
                                   bias=nsq[:, bass.ds(it, 1)], scale=2.0).then_inc(key_ev, 1)

            act.wait_ge(t_ready, UNITS1)
            for par in range(2):
                leave(par, par)
            with act.Fori(1, TILES // 2) as pair:
                for par in range(2):
                    leave(pair * 2 + par, par)
            vals_f = vals[:].rearrange("p t k -> p (t k)")
            act.wait_ge(s_arg, 1)
            act.activation(vals_f, vals_f, ACT.Sqrt).then_inc(s_root, 1)
            act.wait_ge(s_root, 1)
            act.activation(vals_f, vals_f, ACT.Exp, scale=-0.5).then_inc(s_exp, 1)
            act.wait_ge(deg2, 1)
            act.activation(tmp32[:], tmp32[:], ACT.Sqrt).then_inc(deg2_root, 1)

            def evacuate(g, bank, base_unit, base_z):
                act.wait_ge(t_used, g * GROUPS + (base_unit + GROUPS))
                act.wait_ge(z_mm, g + base_z)
                act.wait_ge(z_done, g + base_z)
                act.activation(out_t_m, by_block(acc[bank]), ACT.Copy).then_inc(acc_read, 1)

            def finish_second(g):
                act.wait_ge(var_ready, g + 2)
                act.activation(tmp32[:, 0:U], tmp32[:, 0:U], ACT.Sqrt).then_inc(sd_done, 1)
                act.wait_ge(kept, g + 1)
                act.wait_ge(zt_mm, g + GROUPS)
                wait_alone(act, z_done, g + (GROUPS + 1))
                for u in range(U):
                    ins = act.activation(z_st[:, u], xs[:, bass.ds(g + GROUPS * u, 1), :].rearrange("p o f -> p (o f)"), ACT.Relu,
                                         bias=negmr[:, u:u + 1], scale=tmp32[:, u:u + 1])
                ins.then_inc(h2_done, 1)
                act.wait_ge(zt_mm, g + (GROUPS + 1))
                act.wait_ge(q_mm, g + GROUPS)
                act.activation(flat(t_st[:]), ps_t, ACT.Copy).then_inc(zt_ev, 1)

            evacuate(0, 0, UNITS1, GROUPS)
            finish_second(0)
            evacuate(1, 1, UNITS1, GROUPS)
            with act.Fori(1, GROUPS // 2) as pair:
                for i in range(2):
                    finish_second(pair * 2 + (i - 1))
                    evacuate(pair * 2 + i, i, UNITS1, GROUPS)
            finish_second(GROUPS - 1)

            def store(g, i):
                act.wait_ge(z_done, g + (2 * GROUPS + 1))
                src = (z_st, t_st)[i]
                for q in range(QD):
                    dst = out_v[q, :, g] if isinstance(g, int) else out_v[q, :, bass.ds(g, 1)].rearrange("s o u f -> s (o u) f")
                    act.dma_start(dst, src[R * q:R * q + R]).then_inc(z_out[i], DMA)

            evacuate(0, 0, UNITS1 + UNITS, 2 * GROUPS)
            store(0, 0)
            evacuate(1, 1, UNITS1 + UNITS, 2 * GROUPS)
            with act.Fori(1, GROUPS // 2) as pair:
                for i in range(2):
                    store(pair * 2 + (i - 1), 1 - i)
                    evacuate(pair * 2 + i, i, UNITS1 + UNITS, 2 * GROUPS)
            store(GROUPS - 1, 1)

        @block.vector
        def _(v):
            count = [0]

            def link(ins):
                count[0] += 1
                ins.then_inc(dve, 1)
                v.wait_ge(dve, count[0])

            v.memset(ident[:], 0.0).then_inc(const_st, 1)
            v.memset(fold[:], 0.0).then_inc(const_st, 1)
            v.memset(neghalf[:], -0.5).then_inc(const_st, 1)
            link(v.memset(pick[:].bitcast(F32), 0.0))
            v.memset(pick[0:1].bitcast(F32), 1.0)
            v.memset(pick[R:R + 1].bitcast(F32), 1.0)
            v.memset(sq_rows[2 * R:P].bitcast(F32), 0.0)
            v.wait_ge(x_in, QD * DMA)
            for t in range(TILES):
                ins = v.bn_stats(out=stats[:, t], in_=xs[:, t])
            link(ins)
            for t in range(TILES):
                ins = v.bn_aggr(out=mv[:, t], in_=stats[:, t])
            link(ins)
            v.tensor_scalar(tmp32[:], mv[:, :, 1], LN_EPS, None, ALU.add).then_inc(var_ready, 1)
            v.wait_ge(sqrt_done, 1)
            link(v.reciprocal(tmp32[:], tmp32[:]))
            v.scalar_tensor_tensor(negmr[:], mv[:, :, 0], -1.0, tmp32[:], ALU.mult, ALU.mult).then_inc(ln_ready, 1)

            def transposed(out, slot, off, tiles):
                src = araw[:, slot, :, off:off + tiles * R].rearrange("p m (t s) -> p t m s", s=R)
                return v.transpose(out.rearrange("p t (m s) -> p t m s", s=R), src)

            k = 0

            def unit(slot, first, tiles):
                nonlocal k
                if k >= RING1:
                    v.wait_ge(t_used, k - RING1 + 1)
                transposed(tr[:, k % RING1, 0:tiles], slot, first * R, tiles).then_inc(t_ready, 1)
                k += 1

            n_sums = 0
            for n, (g, c, pieces) in enumerate(part_a):
                def sums():
                    nonlocal n_sums
                    if g >= 2:
                        v.wait_ge(deg_mm, g - 1)
                    v.tensor_reduce(part[:, g % 2, c], araw[:, c], axis=AX_X, op=ALU.add).then_inc(part_dve, 1)
                    n_sums += 1

                v.wait_ge(a_in[c], (g + 1) * PER_LOAD)
                if not act_sums(g, c):
                    sums()
                if c == 0 and g >= 1:
                    v.wait_ge(diag_used, g)
                transposed(tr[:, RING1, c:c + 1], c, g * R, 1).then_inc(diag_ready, 1)
                for first, tiles in pieces:
                    unit(c, first, tiles)
                if c == CHUNKS - 1:
                    v.wait_ge(deg_mm, g + 1)
                    for q in range(QD):
                        ins = v.tensor_copy(deg_g[R * q:R * q + R, g], ps_d[R * q:R * q + R, q * U:q * U + U])
                    ins.then_inc(deg_done, 1)
                    v.wait_ge(sqrt_done, g + 2)
                    link(v.reciprocal(dinv_g[:, g], tmp32[:, 0:U]))
                    v.wait_ge(h_done, TILES)
                    v.tensor_tensor(ys_g[:, g], hs_g[:, g], dinv_g[:, g].unsqueeze(2).broadcast_to([P, U, F]), ALU.mult)\
                        .then_inc(y_ready, 1)

            def add_partial(k_f):
                g = F1[k_f]
                v.wait_ge(t_used, units_after[LOADS_A + k_f * CHUNKS - 1])
                v.wait_ge(z_mm, k_f)
                v.tensor_tensor(out_t_m, by_block(acc[(GROUPS + k_f - 1) % 2]), xs_p[k_f], ALU.add).then_inc(acc_read, 1)

            def make_z(k_f):
                g = F1[k_f]
                v.wait_ge(z_mm, k_f + 1)
                if k_f >= 1:
                    v.wait_ge(q_done, k_f)
                    v.wait_ge(zt_mm, k_f)
                    v.wait_ge(sq_done, k_f)
                else:
                    for p in range(2):
                        v.wait_ge(z_out[p], GROUPS // 2 * QD * DMA)
                    v.wait_ge(bias_in, DMA)
                for u in range(U):
                    t = GROUPS * u + g
                    ins = v.scalar_tensor_tensor(z_st[:, u], ps_z[:, u * F:u * F + F], dinv[:, t:t + 1], bias[:], ALU.mult, ALU.add)
                link(ins)
                v.scalar_tensor_tensor(z_st[:], z_st[:], 0.1, z_st[:], ALU.mult, ALU.max).then_inc(z_done, 1)

            def split_z(k_f):
                g = F1[k_f]
                v.wait_ge(zt_ev, k_f + 1)
                v.tensor_tensor(zt_lo_g[:, g], ps_t.rearrange("p (u q s) -> p u q s", u=U, q=QD),
                                zt_hi_g[:, g].bitcast(F32), ALU.subtract).then_inc(zl_done, 1)

            def split_sq(k_f):
                g = F1[k_f]
                v.wait_ge(qh_done, 2 * k_f + 2)
                v.tensor_tensor(sq_rows_g[R:2 * R, g], ps_q[R:2 * R].rearrange("p (u q s) -> p u q s", u=U, q=QD),
                                z_st[R:2 * R].rearrange("p u (q s) -> p u q s", s=R), ALU.subtract).then_inc(q_done, 1)

            xs_p = [None] + [xs_g[:, g].rearrange("p Q (u r) -> p Q u r", u=U) for g in F1[1:]]
            for j, g in enumerate(F1[1:]):
                loads = part_b[j * CHUNKS:j * CHUNKS + CHUNKS]
                st = stages_first(sum(len(p) for _, _, p in loads))
                i = 0
                for _, c, pieces in loads:
                    v.wait_ge(a_in[c], (GROUPS + j + 1) * PER_LOAD)
                    for first, tiles in pieces:
                        unit(c, first - (g + 1), tiles)
                        if i == st["sum_"] and j >= 1:
                            add_partial(j)
                        if i == st["a2"]:
                            make_z(j)
                        if i == st["b2"]:
                            split_z(j)
                        if i == st["c2"]:
                            split_sq(j)
                        i += 1
            add_partial(GROUPS - 1)
            make_z(GROUPS - 1)
            split_z(GROUPS - 1)
            split_sq(GROUPS - 1)
            v.wait_ge(sq_done, GROUPS)
            v.tensor_scalar(nsq[:], nsq[:], -1.0, None, ALU.mult).then_inc(nsq_done, 1)

            def search(it, par):
                if not (isinstance(it, int) and it < 2):
                    v.wait_ge(top_kept, (it - 1) * 2)
                wait_alone(v, key_ev, it * 4 + 4)
                v.max(m8[:, par], keys[par]).then_inc(dve, 1)
                wait_alone(v, dve, it + (count[0] + 1))
                v.max_index(i8[:, par], m8[:, par], keys[par]).then_inc(max_done, 1)

            for par in range(2):
                search(par, par)
            with v.Fori(1, TILES // 2) as pair:
                for par in range(2):
                    search(pair * 2 + par, par)
            count[0] += TILES
            vals_f = vals[:].rearrange("p t k -> p (t k)")
            v.wait_ge(top_kept, 2 * TILES)
            link(v.tensor_scalar(vals_f, vals_f, -1.0, 0.0, ALU.mult, ALU.max))
            v.tensor_scalar(vals_f, vals_f, 1e-10, None, ALU.add).then_inc(s_arg, 1)

            def product_unit(g, j, base_load, base_unit, place=None):
                place = j if place is None else place
                c, half = divmod(j, CHUNK_UNITS)
                if half == 0:
                    v.wait_ge(a_in[c], (g + (base_load // SLOTS + 1)) * PER_LOAD)
                v.wait_ge(t_used, g * GROUPS + (base_unit + place - TSLOTS + 1))
                transposed(tr[:, place % TSLOTS], c, half * UNIT_COLS, U).then_inc(t_ready, 1)

            for j in range(2):
                product_unit(0, j, LOADS1, UNITS1)
            v.wait_ge(s_exp, 1)
            link(v.tensor_reduce(tmp32[:], vals[:], axis=AX_X, op=ALU.add))
            v.tensor_tensor(tmp32[:], tmp32[:], deg[:], ALU.add).then_inc(deg2, 1)
            v.wait_ge(deg2_root, 1)
            link(v.reciprocal(dinv[:], tmp32[:]))
            for j in range(GROUPS):
                sl = slice(j * U, j * U + U)
                v.tensor_tensor(ys[:, sl], hs[:, sl], dinv[:, sl].unsqueeze(2).broadcast_to([P, U, F]), ALU.mult).then_inc(y_ready, 1)
            v.wait_ge(y_ready, 2 * GROUPS)
            v.wait_ge(hw_in, QD * DMA)
            v.tensor_tensor(hs[:], hw_sb, dinv[:].unsqueeze(2).broadcast_to([P, TILES, F]), ALU.mult).then_inc(gw_ready, 1)
            v.wait_ge(gw_ready, 1)

            base2 = count[0]
            PER_FINISH2 = TOPK - 1

            def finish_second_a(g, i):
                v.wait_ge(z_mm, g + (GROUPS + 1))
                v.wait_ge(gath_in[i], (g - i) * (GATHER // 2) + GATHER)
                for kk in range(TOPK):
                    for u in range(U):
                        s_k = vals[:, bass.ds(g + GROUPS * u, 1), kk:kk + 1].rearrange("p o k -> p (o k)")
                        own = out_t[:, u * F:u * F + F]
                        before = ps_z[:, u * F:u * F + F] if kk == 0 else own
                        ins = v.scalar_tensor_tensor(own, gath[:, i, u, kk], s_k, before, ALU.mult, ALU.add)
                    if kk < TOPK - 1:
                        ins.then_inc(dve, 1)
                        v.wait_ge(dve, g * PER_FINISH2 + (base2 + kk + 1))
                ins.then_inc(gath_used, 1)
                v.wait_ge(gath_used, g + 1)
                for u in range(U):
                    x_u = xs[:, bass.ds(g + GROUPS * u, 1), :].rearrange("p o f -> p (o f)")
                    ins = v.scalar_tensor_tensor(x_u, out_t[:, u * F:u * F + F], dinv[:, bass.ds(g + GROUPS * u, 1)], x_u, ALU.mult, ALU.add)
                ins.then_inc(x1_done, 1)
                wait_alone(v, x1_done, g + 1)
                for u in range(U):
                    ins = v.bn_stats(out=stats4[:, u], in_=xs[:, bass.ds(g + GROUPS * u, 1), :].rearrange("p o f -> p (o f)"))
                ins.then_inc(stats_done, 1)
                wait_alone(v, stats_done, g + 1)
                for u in range(U):
                    ins = v.bn_aggr(out=mv[:, u], in_=stats4[:, u])
                ins.then_inc(aggr_done, 1)
                v.wait_ge(zt_ev, g + GROUPS)
                v.wait_ge(aggr_done, g + 1)
                v.tensor_scalar(tmp32[:, 0:U], mv[:, 0:U, 1], LN_EPS, None, ALU.add).then_inc(var_ready, 1)

            def finish_second_b(g):
                v.wait_ge(sd_done, g + 1)
                v.reciprocal(tmp32[:, 0:U], tmp32[:, 0:U]).then_inc(rsd_done, 1)
                v.wait_ge(rsd_done, g + 1)
                v.scalar_tensor_tensor(negmr[:, 0:U], mv[:, 0:U, 0], -1.0, tmp32[:, 0:U], ALU.mult, ALU.mult).then_inc(z_done, 1)

            def finish_second_c(g):
                v.wait_ge(xb_ready, g + 1)
                v.wait_ge(q_mm, g + (GROUPS + 1))
                x_g = xs_g[:, g] if isinstance(g, int) else xs_g[:, bass.ds(g, 1)].rearrange("p o u f -> p (o u) f")
                v.tensor_tensor(x_g, ps_q.rearrange("p (u f) -> p u f", u=U), x_g, ALU.add).then_inc(q_done, 1)

            def group_second(g, i, prev, before, first=0):
                for j in range(first, GROUPS):
                    product_unit(g, j, LOADS1, UNITS1)
                    if j == 3 and before is not None:
                        finish_second_c(before)
                    if prev is not None:
                        if j == 6:
                            finish_second_a(prev, 1 - i)
                        if j == 7:
                            finish_second_b(prev)

            def finish_third(g, i):
                v.wait_ge(z_mm, g + (2 * GROUPS + 1))
                if isinstance(g, int):
                    src = xs_g[:, g]
                    v.wait_ge(z_out[i], GROUPS // 2 * QD * DMA)
                else:
                    src = xs_g[:, bass.ds(g, 1)].rearrange("p o u f -> p (o u) f")
                    v.wait_ge(z_out[i], (g - i) * (QD * DMA // 2) + GROUPS // 2 * QD * DMA)
                v.tensor_tensor((z_st, t_st)[i][:], ps_z.rearrange("p (u f) -> p u f", u=U), src, ALU.add).then_inc(z_done, 1)

            def group_third(g, i, prev):
                for j in range(GROUPS):
                    product_unit(g, j, LOADS1 + GROUPS * CHUNKS, UNITS1 + UNITS)
                    if j == 2 and isinstance(g, int):
                        finish_second_c(GROUPS - 1)
                    if j == 3:
                        finish_third(prev, 1 - i)

            group_second(0, 0, None, None, first=2)
            group_second(1, 1, 0, None)
            with v.Fori(1, GROUPS // 2) as pair:
                for i in range(2):
                    group_second(pair * 2 + i, i, pair * 2 + (i - 1), pair * 2 + (i - 2))
            for place, j in enumerate(EVENS_FIRST):
                product_unit(0, j, LOADS1 + GROUPS * CHUNKS, UNITS1 + UNITS, place)
                if place == 2:
                    finish_second_a(GROUPS - 1, 1)
                    finish_second_b(GROUPS - 1)
                    finish_second_c(GROUPS - 2)
            group_third(1, 1, 0)
            with v.Fori(1, GROUPS // 2) as pair:
                for i in range(2):
                    group_third(pair * 2 + i, i, pair * 2 + (i - 1))
            v.wait_ge(z_mm, 3 * GROUPS)
            v.wait_ge(z_out[1], (GROUPS - 1) * QD * DMA)
            v.tensor_tensor(t_st[:], ps_z.rearrange("p (u f) -> p u f", u=U), xs_g[:, GROUPS - 1], ALU.add).then_inc(z_done, 1)

        @block.tensor
        def _(pe):
            pe.wait_ge(consts, CONSTS)
            pe.wait_ge(w_in, 3 * DMA)
            pe.transpose(ps_z[:, 0:F], w_raw[:, 0:F], ident[:])
            pe.transpose(ps_z[:, F:2 * F], w_raw[:, F:2 * F], ident[:]).then_inc(wt_mm, 1)

            def four(dst, lhs, rhs):
                for u in range(U):
                    ins = pe.matmul(dst[:, u * F:u * F + F], lhs[:, u * P:u * P + P], rhs, start=True, stop=True)
                return ins

            def transposes(dst, src):
                for u in range(U):
                    ins = pe.transpose(dst[:, u * F:u * F + F], src(u), ident[:])
                return ins

            def first_unit(c, first, tiles, bank, start, stop):
                nonlocal k
                pe.wait_ge(t_ready, k + 1)
                for i in range(tiles):
                    ins = pe.matmul(acc[bank], ys[:, c * GROUPS + first + i], tr[:, k % RING1, i],
                                    start=start and i == 0, stop=stop and i == tiles - 1)
                ins.then_inc(t_used, 1)
                k += 1

            k = 0
            for n, (g, c, pieces) in enumerate(part_a):
                if c == 0:
                    pe.wait_ge(h_done, (g + 1) * U)
                    if g >= 1:
                        pe.wait_ge(ht_ev, g)
                    transposes(ps_t, lambda u: hs[:, GROUPS * u + g]).then_inc(ht_mm, 1)
                    if g >= 2:
                        pe.wait_ge(acc_read, g - 1)
                if c == CHUNKS - 1:
                    pe.wait_ge(ht_ev, g + 1)
                    if g >= 1:
                        pe.wait_ge(hw_ev, g)
                    four(ps_q, flat(t_st[:]), w2s[:]).then_inc(hw_mm, 1)
                    pe.wait_ge(part_dve, consumed[n][2])
                    pe.wait_ge(part_act, consumed[n][3])
                    if g >= 1:
                        pe.wait_ge(deg_done, g)
                    for cc in range(CHUNKS):
                        ins = pe.matmul(ps_d[:, 0:U * QD], fold[:], part[:, g % 2, cc], start=cc == 0, stop=cc == CHUNKS - 1)
                    ins.then_inc(deg_mm, 1)
                for p, (first, tiles) in enumerate(pieces):
                    first_unit(c, first, tiles, g % 2, c == 0 and p == 0, False)
                if c == CHUNKS - 1:
                    pe.wait_ge(diag_ready, (g + 1) * CHUNKS)
                    pe.wait_ge(y_ready, g + 1)
                    for cc in range(CHUNKS):
                        ins = pe.matmul(acc[g % 2], ys[:, cc * GROUPS + g], tr[:, RING1, cc],
                                        start=g == 0 and cc == 0, stop=cc == CHUNKS - 1)
                    ins.then_inc(diag_used, 1)

            def finish_first_a(k_f):
                pe.wait_ge(acc_read, GROUPS + k_f)
                if k_f >= 1:
                    pe.wait_ge(z_done, k_f)
                four(ps_z, out_t[:], w1s[:]).then_inc(z_mm, 1)

            def finish_first_b(k_f):
                pe.wait_ge(z_done, k_f + 1)
                if k_f >= 1:
                    pe.wait_ge(zl_done, k_f)
                transposes(ps_t, lambda u: z_st[:, u]).then_inc(zt_mm, 1)

            def finish_first_c(k_f):
                pe.wait_ge(zt_ev, k_f + 1)
                if k_f >= 1:
                    pe.wait_ge(q_done, k_f)
                pe.matmul(ps_q, neghalf[:], flat(t_st[:]), start=True, stop=True).then_inc(q_mm, 1)

            for j, g in enumerate(F1[1:]):
                loads = part_b[j * CHUNKS:j * CHUNKS + CHUNKS]
                n_units = sum(len(p) for _, _, p in loads)
                st = stages_first(n_units)
                i = 0
                pe.wait_ge(acc_read, GROUPS + j - 1)
                for _, c, pieces in loads:
                    for first, tiles in pieces:
                        first_unit(c, first, tiles, (GROUPS + j) % 2, i == 0, i == n_units - 1)
                        if i == st["a"]:
                            finish_first_a(j)
                        if i == st["b"]:
                            finish_first_b(j)
                        if i == st["c"]:
                            finish_first_c(j)
                        i += 1
            finish_first_a(GROUPS - 1)
            finish_first_b(GROUPS - 1)
            finish_first_c(GROUPS - 1)

            def distances(it, par):
                pe.wait_ge(zs_ready, it * 2 + 2)
                for c in range(8):
                    cols = slice(c * 512, c * 512 + 512)
                    if c % 2 == 0 and not (isinstance(it, int) and it < 1):
                        pe.wait_ge(key_ev, it * 4 + (c // 2 - 3))
                    zh = zt_hi[:].rearrange("p q t s -> p (q t s)")[:, cols]
                    zl = zt_lo[:].rearrange("p q t s -> p (q t s)")[:, cols]
                    sq = sq_rows[:].rearrange("p q t s -> p (q t s)")[:, cols]
                    pe.matmul(ps[:, c], pick[:], sq, start=True, stop=False)
                    pe.matmul(ps[:, c], zs_hi[:, par], zl, start=False, stop=False)
                    pe.matmul(ps[:, c], zs_lo[:, par], zh, start=False, stop=False)
                    ins = pe.matmul(ps[:, c], zs_hi[:, par], zh, start=False, stop=True)
                    if c % 2:
                        ins.then_inc(bank_mm, 1)

            pe.wait_ge(q_done, GROUPS)
            for par in range(2):
                distances(par, par)
            with pe.Fori(1, TILES // 2) as pair:
                for par in range(2):
                    distances(pair * 2 + par, par)

            def unit(g, j, bank, base_unit, src):
                pe.wait_ge(t_ready, g * GROUPS + (base_unit + j + 1))
                for i in range(U):
                    ins = pe.matmul(acc[bank], src[:, j * U + i], tr[:, j % TSLOTS, i],
                                    start=j == 0 and i == 0, stop=j == GROUPS - 1 and i == U - 1)
                ins.then_inc(t_used, 1)

            def finish_second_a(g):
                pe.wait_ge(acc_read, g + 2 * GROUPS)
                pe.wait_ge(z_done, g + GROUPS)
                four(ps_z, out_t[:], w2s[:]).then_inc(z_mm, 1)

            def finish_second_b(g):
                pe.wait_ge(h2_done, g + 1)
                pe.wait_ge(zt_ev, g + GROUPS)
                transposes(ps_t, lambda u: z_st[:, u]).then_inc(zt_mm, 1)

            def finish_second_c(g):
                pe.wait_ge(zt_ev, g + (GROUPS + 1))
                pe.wait_ge(q_done, g + GROUPS)
                four(ps_q, flat(t_st[:]), ws_t[:]).then_inc(q_mm, 1)

            def group_second(g, i, prev, before):
                pe.wait_ge(acc_read, g + (2 * GROUPS - 2))
                for j in range(GROUPS):
                    if isinstance(g, int) and g == 0:
                        pe.wait_ge(y_ready, GROUPS + j + 1)
                    unit(g, j, i, UNITS1, ys)
                    if j == 0 and before is not None:
                        finish_second_b(before)
                    if j == 1 and before is not None:
                        finish_second_c(before)
                    if j == 2 and prev is not None:
                        finish_second_a(prev)

            def finish_third(g):
                pe.wait_ge(acc_read, g + 3 * GROUPS)
                pe.wait_ge(z_done, g + 2 * GROUPS)
                four(ps_z, out_t[:], wn_t[:]).then_inc(z_mm, 1)

            def group_third(g, i, prev):
                pe.wait_ge(acc_read, g + (3 * GROUPS - 2))
                for j in range(GROUPS):
                    unit(g, j, i, UNITS1 + UNITS, hs)
                    if prev is not None and j == 0:
                        finish_third(prev)

            pe.wait_ge(key_ev, 4 * TILES)
            group_second(0, 0, None, None)
            group_second(1, 1, 0, None)
            with pe.Fori(1, GROUPS // 2) as pair:
                for i in range(2):
                    group_second(pair * 2 + i, i, pair * 2 + (i - 1), pair * 2 + (i - 2))
            pe.wait_ge(acc_read, 3 * GROUPS - 2)
            pe.wait_ge(kept, U + 1)
            finish_second_b(GROUPS - 2)
            for place in range(TSLOTS):
                pe.wait_ge(t_ready, UNITS1 + UNITS + place + 1)
                for i in range(U):
                    ins = pe.matmul(acc[0], hs[:, EVENS_FIRST[place] * U + i], tr[:, place, i],
                                    start=place == 0 and i == 0, stop=False)
                ins.then_inc(t_used, 1)
                if place == 0:
                    finish_second_c(GROUPS - 2)
                    finish_second_a(GROUPS - 1)
            for i in range(U):
                pe.wait_ge(kept, U + i + 2)
                for place in range(TSLOTS, GROUPS):
                    if i == 0:
                        pe.wait_ge(t_ready, UNITS1 + UNITS + place + 1)
                    ins = pe.matmul(acc[0], hs[:, EVENS_FIRST[place] * U + i], tr[:, place - TSLOTS, i],
                                    start=False, stop=i == U - 1 and place == GROUPS - 1)
                    if i == U - 1:
                        ins.then_inc(t_used, 1)
                if i == 1:
                    finish_second_b(GROUPS - 1)
                if i == U - 1:
                    finish_second_c(GROUPS - 1)
            group_third(1, 1, 0)
            with pe.Fori(1, GROUPS // 2) as pair:
                for i in range(2):
                    group_third(pair * 2 + i, i, pair * 2 + (i - 1))
            finish_third(GROUPS - 1)


_INS = ['x', 'adj', 'L0_gnn_W1', 'L0_gnn_b1', 'L0_gnn_W2', 'L0_gnn_b2', 'L1_gnn_W', 'L1_gnn_b']
_OUTS = [((N, F), 'float32')]


def kernel(**inputs):
    import numpy as _np
    import concourse.bacc as _bacc
    from concourse import mybir as _mybir
    from concourse.bass_utils import run_bass_kernel_spmd as _run

    nc = _bacc.Bacc("TRN2", target_bir_lowering=False, num_devices=1)
    arrays, args = {}, []
    for name in _INS:
        a = _np.ascontiguousarray(inputs[name])
        arrays[f"in_{name}_dram"] = a
        args.append(nc.dram_tensor(f"in_{name}_dram", a.shape, _mybir.dt.from_np(a.dtype), kind="ExternalInput").ap())
    for i, (shape, dtype) in enumerate(_OUTS):
        args.append(nc.dram_tensor(f"out_{i}_dram", shape, _mybir.dt.from_np(_np.dtype(dtype)), kind="ExternalOutput").ap())
    gnn_kernel(nc, *args)
    r = _run(nc, [arrays], core_ids=[0])
    return r.results[0]["out_0_dram"]
```

```python
from contextlib import ExitStack

import concourse.bass as bass
from concourse import mybir

F32 = mybir.dt.float32
F32R = mybir.dt.float32r
U32 = mybir.dt.uint32
ACT = mybir.ActivationFunctionType
ALU = mybir.AluOpType
AX_X = mybir.AxisListType.X

N = 4096
F = 128
P = 128
QD = 4
R = 32
TILES = N // P
U = 4
GROUPS = TILES // U
GI = U * P
UNIT_COLS = U * R
CHUNK_UNITS = 2
CHUNK_COLS = CHUNK_UNITS * UNIT_COLS
CHUNKS = GROUPS // CHUNK_UNITS
SLOTS = 4
TSLOTS = 4
TOPK = 4
LN_EPS = 1e-5
DMA = 16


def gnn_kernel(nc, x, adj, W1, b1, W2, b2, W, b, out):
    x_v = x.rearrange("(q t s) f -> q s t f", q=QD, t=TILES)
    out_v = out.rearrange("(q u g s) f -> q s g u f", q=QD, g=GROUPS, u=U)
    adj_v = adj.rearrange("(m g r) (q c) -> q r g m c", m=QD * U, g=GROUPS, q=QD)
    hw_dram = nc.dram_tensor("hw_scratch", (N, F), F32).ap()
    table = nc.dram_tensor("neighbour_table", (N, F), F32).ap()
    keys_dram = nc.dram_tensor("keys_scratch", (P * TILES, F), F32).ap()
    keys_lane = keys_dram.rearrange("(p b) f -> p (b f)", p=P)
    hw_v = hw_dram.rearrange("(q u g s) f -> q s g u f", q=QD, g=GROUPS, u=U)
    hw_tv = hw_dram.rearrange("(q t s) f -> q s t f", q=QD, t=TILES)
    table_v = table.rearrange("(q t s) f -> q s t f", q=QD, t=TILES)

    ctx = ExitStack()
    with ctx:
        def sb(name, shape, dt=F32):
            return ctx.enter_context(nc.sbuf_tensor(name, shape, dt))

        def sem(name):
            return ctx.enter_context(nc.semaphore(name))

        araw = sb("araw", [P, SLOTS, U * QD, CHUNK_COLS])
        tr = sb("tr", [P, TSLOTS, U, GI])
        xs = sb("xs", [P, TILES, F])
        hs = sb("hs", [P, TILES, F])
        ys = sb("ys", [P, TILES, F])
        zt_hi = sb("zt_hi", [P, QD, TILES, R], F32R)
        zt_lo = sb("zt_lo", [P, QD, TILES, R], F32R)
        sq_rows = sb("sq_rows", [P, QD, TILES, R], F32R)
        out_t = sb("out_t", [P, GI])
        z_st = sb("z_st", [P, U, F])
        t_st = sb("t_st", [P, U, F])
        zs_hi = sb("zs_hi", [P, 2, P], F32R)
        zs_lo = sb("zs_lo", [P, 2, P], F32R)
        w1s = sb("w1s", [F, F])
        w2s = sb("w2s", [F, F])
        ws_t = sb("ws_t", [F, F])
        wn_t = sb("wn_t", [F, F])
        bias = sb("bias", [P, F])
        ident = sb("ident", [P, P])
        fold = sb("fold", [P, P])
        neghalf = sb("neghalf", [P, P])
        pick = sb("pick", [P, P], F32R)
        part = sb("part", [P, 2, CHUNKS, U * QD])
        deg = sb("deg", [P, TILES])
        dinv = sb("dinv", [P, TILES])
        root_deg = sb("root_deg", [P, U])
        tmp32 = sb("tmp32", [P, TILES])
        mv = sb("mv", [P, TILES, 2])
        negmr = sb("negmr", [P, TILES])
        nsq = sb("nsq", [P, TILES])
        vals = sb("vals", [P, TILES, TOPK])
        idx = sb("idx", [P, TILES, TOPK], U32)
        m8 = sb("m8", [P, 2, 8])
        i8 = sb("i8", [P, 2, 8], U32)
        bmax = sb("bmax", [P, TILES])
        bm8 = sb("bm8", [P, 8])
        bi8 = sb("bi8", [P, 8], U32)
        lane_rows = sb("lane_rows", [P, 1])
        block_row = sb("block_row", [P, TOPK], U32)
        idx_st = sb("idx_st", [P, 2, U * TOPK], U32)
        stats4 = sb("stats4", [P, U, 6])

        xs_g = xs[:].rearrange("p (u g) f -> p g u f", g=GROUPS)
        hs_g = hs[:].rearrange("p (u g) f -> p g u f", g=GROUPS)
        ys_g = ys[:].rearrange("p (u g) f -> p g u f", g=GROUPS)
        deg_g = deg[:].rearrange("p (u g) -> p g u", g=GROUPS)
        dinv_g = dinv[:].rearrange("p (u g) -> p g u", g=GROUPS)
        idx_even = idx[:].rearrange("p (i two) k -> p i two k", two=2)[:, :, 0]
        idx_g = idx[:].rearrange("p (u g) k -> p g u k", g=GROUPS)
        zt_hi_g = zt_hi[:].rearrange("p q (u g) s -> p g u q s", g=GROUPS)
        zt_lo_g = zt_lo[:].rearrange("p q (u g) s -> p g u q s", g=GROUPS)
        sq_rows_g = sq_rows[:].rearrange("p q (u g) s -> p g u q s", g=GROUPS)
        out_t_m = out_t[:].rearrange("p (u Q r) -> p Q u r", u=U, Q=QD)

        def by_block(flat):
            return flat.rearrange("p (Q u r) -> p Q u r", Q=QD, u=U)

        xs_m = [xs_g[:, g].rearrange("p u (Q r) -> p Q u r", r=R) for g in range(GROUPS)]
        stats = out_t[:, 2 * F:2 * F + TILES * 6].rearrange("p (t k) -> p t k", k=6)
        w_raw = out_t[:, 0:2 * F]
        keys = [araw[:, 2 + i].rearrange("p c k -> p (c k)") for i in range(2)]
        ring1 = tr[:].rearrange("p a b k -> p (a b) k")
        hw_sb = tr[:, 2:4].rearrange("p a b (c f) -> p (a b c) f", f=F)
        blocks, place, key_place, beyond, step = [
            z_st[:, i // 2].rearrange("p (h t k) -> p h t k", h=2, k=TOPK)[:, i % 2] for i in range(5)]
        step = step[:, :, 0:TOPK - 1]
        cand = t_st[:]
        cand_f = t_st[:].rearrange("p k f -> p (k f)")
        gath = zt_lo[:].bitcast(F32).rearrange("p q t s -> p (q t s)")\
            .rearrange("p (i u k f) -> p i u k f", i=2, u=U, k=TOPK)

        y_hi, y_lo = [zt_hi[:].rearrange("p q t s -> p (q t s)").rearrange("p (h g u f) -> p h g u f", h=2, g=U, u=U)[:, h]
                      for h in range(2)]
        tr_hi, tr_lo = [b[:].rearrange("p q t s -> p (q t s)").rearrange("p (i u k) -> p i u k", i=2, u=U)
                        for b in (zt_lo, sq_rows)]

        ps = ctx.enter_context(nc.psum_tensor("ps", [P, 8, 512], F32))
        acc = [ps[:, 0], ps[:, 1]]
        ps_z = ps[:, 2]
        ps_t = ps[:, 3]
        ps_q = ps[:, 4]
        ps_d = ps[:, 5]
        junk = [ps[:, 6], ps[:, 7]]

        x_in = sem("x_in")
        w_in = sem("w_in")
        bias_in = sem("bias_in")
        consts = sem("consts")
        const_st = sem("const_st")
        a_in = [sem(f"a_in{i}") for i in range(SLOTS)]
        t_ready = sem("t_ready")
        t_used = sem("t_used")
        diag_ready = sem("diag_ready")
        diag_used = sem("diag_used")
        part_dve = sem("part_dve")
        part_act = sem("part_act")
        acc_read = sem("acc_read")
        deg_mm = sem("deg_mm")
        deg_done = sem("deg_done")
        sqrt_done = sem("sqrt_done")
        y_ready = sem("y_ready")
        var_ready = sem("var_ready")
        ln_ready = sem("ln_ready")
        h_done = sem("h_done")
        ht_mm = sem("ht_mm")
        ht_ev = sem("ht_ev")
        hw_mm = sem("hw_mm")
        hw_ev = sem("hw_ev")
        z_out = [sem("z_out0"), sem("z_out1")]
        hw_in = sem("hw_in")
        wt_mm = sem("wt_mm")
        wt_ev = sem("wt_ev")
        z_mm = sem("z_mm")
        z_done = sem("z_done")
        sq_done = sem("sq_done")
        zt_mm = sem("zt_mm")
        zt_ev = sem("zt_ev")
        zl_done = sem("zl_done")
        q_mm = sem("q_mm")
        qh_done = sem("qh_done")
        q_done = sem("q_done")
        nsq_done = sem("nsq_done")
        zs_ready = sem("zs_ready")
        bank_mm = sem("bank_mm")
        key_ev = sem("key_ev")
        max_done = sem("max_done")
        top_kept = sem("top_kept")
        x_b2 = sem("x_b2")
        y_hi_done = sem("y_hi_done")
        y_lo_done = sem("y_lo_done")
        hi_done = sem("hi_done")
        lo_done = sem("lo_done")
        lane_max = sem("lane_max")
        lane_found = sem("lane_found")
        block_maxima = sem("block_maxima")
        best_blocks = sem("best_blocks")
        block_places = sem("block_places")
        rows_ready = sem("rows_ready")
        blocks_kept = sem("blocks_kept")
        keys_out = sem("keys_out")
        cand_in = sem("cand_in")
        cand_max = sem("cand_max")
        cand_used = sem("cand_used")
        decode = sem("decode")
        s_arg = sem("s_arg")
        s_root = sem("s_root")
        s_exp = sem("s_exp")
        deg2 = sem("deg2")
        deg2_root = sem("deg2_root")
        gw_ready = sem("gw_ready")
        table_out = sem("table_out")
        x_again = sem("x_again")
        idx_ready = sem("idx_ready")
        gath_in = [sem("gath_in0"), sem("gath_in1")]
        gath_used = sem("gath_used")
        x1_done = sem("x1_done")
        stats_done = sem("stats_done")
        aggr_done = sem("aggr_done")
        rsd_done = sem("rsd_done")
        sd_done = sem("sd_done")
        h2_done = sem("h2_done")
        kept = sem("kept")
        xb_ready = sem("xb_ready")
        chained = sem("chained")
        junk_written = sem("junk_written")

        block = ctx.enter_context(nc.Block())

        RING1 = (TSLOTS - 1) * U
        tiles1 = 0

        def pieces_of(first, end):
            nonlocal tiles1
            pieces = []
            while first < end:
                n = min(U, end - first, RING1 - tiles1 % RING1)
                pieces.append((first, n))
                first += n
                tiles1 += n
            return pieces

        part_a = []
        for g in range(GROUPS):
            for c in range(CHUNKS):
                part_a.append((g, c, pieces_of(0, g)))
        TILES_A = tiles1
        part_b = []
        for g in reversed(range(GROUPS - 1)):
            tiles = GROUPS - 1 - g
            tiles += tiles == 3
            per_slot = min(CHUNKS, GROUPS // tiles) if tiles != U or g == 4 else 1
            for c in range(0, CHUNKS, per_slot):
                part_b.append((g, range(c, c + per_slot), tiles,
                               [pieces_of(g + 1, GROUPS) for _ in range(per_slot)]))
        loads_in = [0] * SLOTS
        arrived = []
        for n in range(len(part_a) + len(part_b)):
            chunks = 1 if n < len(part_a) else len(part_b[n - len(part_a)][1])
            loads_in[n % SLOTS] += chunks * QD * DMA
            arrived.append(loads_in[n % SLOTS])
        LOADS_A, LOADS1 = len(part_a), len(part_a) + len(part_b)
        assert LOADS1 % SLOTS == 0
        UNITS1 = sum(len(p) for _, _, p in part_a) + sum(len(p) for load in part_b for p in load[3])
        UNITS = GROUPS * GROUPS
        USED1 = tiles1
        F1 = [GROUPS - 1] + list(reversed(range(GROUPS - 1)))
        PER_LOAD = QD * DMA
        EVENS_FIRST = list(range(0, GROUPS, 2)) + list(range(1, GROUPS, 2))
        CAND = TOPK * DMA
        GATHER = U * TOPK * DMA
        CONSTS = 1 + QD

        def act_sums(g, c):
            return c != CHUNKS - 1 and (c != 1 or g >= 5)

        consumed = []
        k = n_dve = n_act = n_diag = 0
        for g, c, pieces in part_a:
            k += len(pieces)
            n_diag += 1
            n_act += act_sums(g, c)
            n_dve += not act_sums(g, c)
            consumed.append((k, n_diag, n_dve, n_act))
        for g, _, _, pieces in part_b:
            k += sum(len(p) for p in pieces)
            consumed.append((k, n_diag, n_dve, n_act))
        ends = [0]
        for g in F1[1:]:
            ends.append(ends[-1] + CHUNKS * (GROUPS - 1 - g))
        LAG = 7
        STAGE_A = [1]
        for k in range(1, GROUPS):
            STAGE_A.append(max(ends[k] + 4, STAGE_A[-1] + 9))
        STAGE_B = [t + 4 for t in STAGE_A]
        STAGE_C = [t + 7 for t in STAGE_A]
        ADD = [t + LAG for t in ends]
        MAKE_Z = [t + LAG for t in STAGE_A]
        SPLIT_Z = [t + 2 + LAG for t in STAGE_B]
        SPLIT_SQ = [t + 2 + LAG for t in STAGE_C]

        def split_units(g, j):
            return g * U + (j // 2 - U)

        LATE = [U <= g < GROUPS - 1 for g in range(GROUPS)]

        def late_diag(g, c, p):
            return g >= 0 and LATE[g] and c == 0 and p == 0

        def wait_alone(eng, signal, value):
            if not isinstance(value, int):
                value = eng.to_reg(value)
                eng.wait_ge(x_in, QD * DMA)
            eng.wait_ge(signal, value)

        def load(sp, slot, g, c0, cols, at=0):
            for q in range(QD):
                if isinstance(g, int):
                    src = adj_v[q, :, g, :, c0:c0 + cols]
                else:
                    src = adj_v[q, :, bass.ds(g, 1), :, c0:c0 + cols].rearrange("r o m c -> r (o m) c")
                sp.dma_start(araw[R * q:R * q + R, slot, :, at:at + cols], src).then_inc(a_in[slot], DMA)

        def flat(x3):
            return x3.rearrange("p u f -> p (u f)")

        @block.sync
        def _(sp):
            for q in range(QD):
                sp.dma_start(xs[R * q:R * q + R], x_v[q]).then_inc(x_in, DMA)
            sp.dma_start(w_raw, W).then_inc(w_in, DMA)
            sp.dma_start(w2s[:], W2).then_inc(w_in, DMA)
            sp.dma_start(w1s[:], W1).then_inc(w_in, DMA)
            sp.dma_start(bias[:], b1.partition_broadcast(P)).then_inc(bias_in, DMA)
            for n in range(LOADS1):
                if n >= SLOTS:
                    was = consumed[n - SLOTS]
                    if was[0]:
                        sp.wait_ge(t_ready, was[0])
                    if n - SLOTS < LOADS_A:
                        sp.wait_ge(diag_ready, was[1])
                        if act_sums(part_a[n - SLOTS][0], part_a[n - SLOTS][1]):
                            sp.wait_ge(part_act, was[3])
                        else:
                            sp.wait_ge(part_dve, was[2])
                if n < LOADS_A:
                    g, c, _ = part_a[n]
                    load(sp, n % SLOTS, g, c * CHUNK_COLS, CHUNK_COLS)
                else:
                    g, chunks, tiles, _ = part_b[n - LOADS_A]
                    for i, c in enumerate(chunks):
                        load(sp, n % SLOTS, g, (c * GROUPS + GROUPS - tiles) * R, tiles * R, i * tiles * R)
            sp.wait_ge(z_mm, GROUPS)
            for q in range(QD):
                sp.dma_start(xs[R * q:R * q + R], x_v[q]).then_inc(x_again, DMA)
            sp.wait_ge(z_done, GROUPS)
            sp.dma_start(bias[:], b2.partition_broadcast(P)).then_inc(bias_in, DMA)

            def keys_store(pair):
                for c in range(4):
                    if c == 0 and not (isinstance(pair, int) and pair == 0):
                        sp.wait_ge(cand_in, pair * CAND)
                    wait_alone(sp, key_ev, pair * 8 + (c + 1))
                    sp.dma_start(keys_lane[:, c * 1024:c * 1024 + 1024], keys[0][:, c * 1024:c * 1024 + 1024]).then_inc(keys_out, DMA)

            keys_store(0)
            sp.wait_ge(t_used, USED1)
            for p in range(2):
                sp.wait_ge(z_out[p], GROUPS // 2 * QD * DMA)
            for q in range(QD):
                sp.dma_start(hw_sb[R * q:R * q + R], hw_tv[q]).then_inc(hw_in, DMA)
            for n in range(SLOTS // 2):
                keys_store(1 + n)
                load(sp, n, 0, n * CHUNK_COLS, CHUNK_COLS)
            with sp.Fori(1 + SLOTS // 2, TILES // 2) as pair:
                keys_store(pair)
            sp.wait_ge(x_b2, TILES // 2 - 1)
            sp.wait_ge(kept, 1)
            sp.dma_start(bias[:], b.partition_broadcast(P)).then_inc(bias_in, DMA)
            sp.wait_ge(keys_out, TILES // 2 * 4 * DMA)
            sp.wait_ge(block_maxima, TILES // 2)
            load(sp, 2, 0, 2 * CHUNK_COLS, CHUNK_COLS)
            sp.wait_ge(max_done, TILES // 2)
            load(sp, 3, 0, 3 * CHUNK_COLS, CHUNK_COLS)
            sp.wait_ge(gw_ready, 1)
            for q in range(QD):
                sp.dma_start(table_v[q], hs[R * q:R * q + R]).then_inc(table_out, DMA)
            def load_group(g2):
                g = g2 % GROUPS if isinstance(g2, int) else sp.snap(g2 % GROUPS)
                for c in range(CHUNKS):
                    taken = CHUNKS + c + 1 if isinstance(g2, int) else (c + 1) * CHUNK_UNITS
                    sp.wait_ge(t_ready, g2 * GROUPS + (UNITS1 + taken - GROUPS))
                    load(sp, c, g, c * CHUNK_COLS, CHUNK_COLS)

            with sp.Fori(1, GROUPS + 1) as g2:
                load_group(g2)
            load_group(GROUPS + 1)
            with sp.Fori(GROUPS + 2, 2 * GROUPS) as g2:
                load_group(g2)
            for p in range(2):
                sp.wait_ge(z_out[p], GROUPS * QD * DMA)

        @block.gpsimd
        def _(gp):
            gp.wait_ge(const_st, 3)
            gp.affine_select(out=ident[:], in_=ident[:], compare_op=ALU.not_equal, fill=1.0, base=0,
                             pattern=[[-1, P]], channel_multiplier=1).then_inc(consts, 1)
            fold_v = fold[:].rearrange("p (a b) -> p a b", b=R)
            for q in range(QD):
                gp.affine_select(out=fold_v, in_=fold_v, compare_op=ALU.not_equal, fill=1.0, base=-R * q,
                                 pattern=[[0, QD], [-1, R]], channel_multiplier=1).then_inc(consts, 1)
                gp.wait_ge(consts, 2 + q)

            def stage_tile(it, par):
                if not (isinstance(it, int) and it < 2):
                    gp.wait_ge(bank_mm, (it - 1) * 4)
                dst_h = zs_hi[:, par].rearrange("p (q s) -> p q s", s=R)
                dst_l = zs_lo[:, par].rearrange("p (q s) -> p q s", s=R)
                gp.tensor_copy(dst_h, zt_hi[:, :, bass.ds(it, 1), :].rearrange("p q o s -> p q (o s)")).then_inc(zs_ready, 1)
                gp.tensor_copy(dst_l, zt_lo[:, :, bass.ds(it, 1), :].rearrange("p q o s -> p q (o s)")).then_inc(zs_ready, 1)

            def read_blocks(pair):
                wait_alone(gp, block_places, pair + 1)
                gp.tensor_scalar(block_row[:], bi8[:, 0:TOPK], lane_rows[:, 0:1], None, ALU.add).then_inc(rows_ready, 1)
                gp.tensor_copy(blocks[:, bass.ds(pair, 1), :].rearrange("p o k -> p (o k)"), bi8[:, 0:TOPK]).then_inc(blocks_kept, 1)
                if not isinstance(pair, int):
                    wait_alone(gp, cand_used, pair)
                wait_alone(gp, rows_ready, pair + 1)
                wait_alone(gp, keys_out, pair * (4 * DMA) + 4 * DMA)
                for kk in range(TOPK):
                    gp.indirect_dma_start(
                        out=cand[:, kk, :], out_offset=None, in_=keys_dram,
                        in_offset=bass.IndirectOffsetOnAxis(ap=block_row[:, kk:kk + 1], axis=0),
                        bounds_check=P * TILES - 1).then_inc(cand_in, DMA)

            def keep_top(it, par, pair):
                if par:
                    gp.wait_ge(max_done, pair + 1)
                else:
                    gp.wait_ge(cand_used, pair + 1)
                gp.tensor_copy(vals[:, bass.ds(it, 1), :].rearrange("p o k -> p (o k)"), m8[:, par, 0:TOPK]).then_inc(top_kept, 1)
                gp.tensor_copy(idx[:, bass.ds(it, 1), :].rearrange("p o k -> p (o k)"), i8[:, par, 0:TOPK]).then_inc(top_kept, 1)

            gp.wait_ge(zl_done, GROUPS)
            for par in range(2):
                stage_tile(par, par)

            def add_bias(pair):
                two = xs[:, bass.ds(pair * 2, 2), :]
                return gp.tensor_tensor(two, two, bias[:].unsqueeze(1).broadcast_to([P, 2, F]), ALU.add)

            gp.wait_ge(x_again, QD * DMA)
            gp.wait_ge(bias_in, 2 * DMA)
            with gp.Fori(1, TILES // 2) as pair:
                stage_tile(pair * 2, 0)
                read_blocks(pair - 1)
                stage_tile(pair * 2 + 1, 1)
                add_bias(pair - 1).then_inc(x_b2, 1)
                for par in (1, 0):
                    keep_top(pair * 2 + (par - 2), par, pair - 1)
            add_bias(TILES // 2 - 1).then_inc(kept, 1)
            read_blocks(TILES // 2 - 1)
            for par in (1, 0):
                keep_top(TILES - 2 + par, par, TILES // 2 - 1)

            n_decode = 0

            def decoded(ins):
                nonlocal n_decode
                n_decode += 1
                ins.then_inc(decode, 1)
                gp.wait_ge(decode, n_decode)

            gp.wait_ge(top_kept, 2 * TILES)
            decoded(gp.tensor_copy(place, idx_even))
            decoded(gp.tensor_scalar(blocks, blocks, float(F), None, ALU.mult))
            decoded(gp.tensor_tensor(step, blocks[:, :, 1:TOPK], blocks[:, :, 0:TOPK - 1], ALU.subtract))
            decoded(gp.tensor_scalar(step, step, -float(F), None, ALU.add))
            decoded(gp.tensor_tensor(key_place, place, blocks[:, :, 0:1].broadcast_to([P, TILES // 2, TOPK]), ALU.add))
            for i in range(1, TOPK):
                decoded(gp.tensor_scalar(beyond, place, float(F * i), None, ALU.is_ge))
                decoded(gp.tensor_tensor(beyond, beyond, step[:, :, i - 1:i].broadcast_to([P, TILES // 2, TOPK]), ALU.mult))
                decoded(gp.tensor_tensor(key_place, key_place, beyond, ALU.add))
            decoded(gp.tensor_copy(idx_even, key_place))

            def gather_group(g, i):
                if not isinstance(g, int):
                    gp.wait_ge(gath_used, g - 1)
                    gp.wait_ge(gath_in[i], (g - i) * (GATHER // 2))
                src = idx_g[:, g] if isinstance(g, int) else idx_g[:, bass.ds(g, 1)].rearrange("p o u k -> p (o u) k")
                gp.tensor_copy(idx_st[:, i].rearrange("p (u k) -> p u k", u=U), src).then_inc(idx_ready, 1)
                wait_alone(gp, idx_ready, g + 1)
                for u in range(U):
                    for k in range(TOPK):
                        gp.indirect_dma_start(
                            out=gath[:, i, u, k, :], out_offset=None, in_=table,
                            in_offset=bass.IndirectOffsetOnAxis(ap=idx_st[:, i, u * TOPK + k:u * TOPK + k + 1], axis=0),
                            bounds_check=N - 1).then_inc(gath_in[i], DMA)

            def keep_h2(g, split):
                gp.wait_ge(h2_done, g + 1)
                dst = hs_g[:, g] if isinstance(g, int) else hs_g[:, bass.ds(g, 1)].rearrange("p o u f -> p (o u) f")
                if split:
                    gs = slice(g, g + 1) if isinstance(g, int) else bass.ds(g, 1)
                    hi, lo = [y[:, gs].rearrange("p o u f -> p (o u) f") for y in (y_hi, y_lo)]
                    gp.tensor_copy(hi, z_st[:]).then_inc(y_hi_done, 1)
                    wait_alone(gp, y_hi_done, g + 1)
                    gp.tensor_tensor(lo, z_st[:], hi.bitcast(F32), ALU.subtract).then_inc(y_lo_done, 1)
                gp.tensor_copy(dst, z_st[:]).then_inc(kept, 1)
                x_g = xs_g[:, g] if isinstance(g, int) else xs_g[:, bass.ds(g, 1)].rearrange("p o u f -> p (o u) f")
                gp.tensor_tensor(x_g, x_g, bias[:].unsqueeze(1).broadcast_to([P, U, F]), ALU.add).then_inc(xb_ready, 1)

            gp.wait_ge(table_out, QD * DMA)
            gp.wait_ge(top_kept, 2 * TILES)
            for i in range(2):
                gather_group(i, i)
            gp.wait_ge(bias_in, 3 * DMA)
            with gp.Fori(1, U // 2 + 1) as pair:
                for i in range(2):
                    keep_h2(pair * 2 + (i - 2), True)
                    gather_group(pair * 2 + i, i)
            with gp.Fori(U // 2 + 1, GROUPS // 2) as pair:
                for i in range(2):
                    keep_h2(pair * 2 + (i - 2), False)
                    gather_group(pair * 2 + i, i)
            for i in range(2):
                keep_h2(GROUPS - 2 + i, False)

            def split_low(g):
                for j in range(0, GROUPS, 2):
                    gp.wait_ge(t_used, g * GROUPS + (USED1 + UNITS + j - 3))
                    wait_alone(gp, hi_done, split_units(g, j) + 1)
                    i = j // 2 % 2
                    gp.tensor_tensor(tr_lo[:, i], tr[:, j % TSLOTS], tr_hi[:, i].bitcast(F32), ALU.subtract).then_inc(lo_done, 1)

            with gp.Fori(1, GROUPS) as g:
                split_low(g)

        @block.scalar
        def _(act):
            act.wait_ge(var_ready, 1)
            act.activation(tmp32[:], tmp32[:], ACT.Sqrt).then_inc(sqrt_done, 1)
            act.wait_ge(ln_ready, 1)

            def normalize(g):
                for u in range(U):
                    t = GROUPS * u + g
                    act.activation(hs[:, t], xs[:, t], ACT.Relu, bias=negmr[:, t:t + 1], scale=tmp32[:, t:t + 1]).then_inc(h_done, 1)

            normalize(0)
            act.wait_ge(wt_mm, 1)
            act.activation(ws_t[:], ps_z[:, 0:F], ACT.Copy).then_inc(wt_ev, 1)
            act.activation(wn_t[:], ps_z[:, F:2 * F], ACT.Copy).then_inc(wt_ev, 1)

            n_sums = 0

            def row_sums(g, c):
                nonlocal n_sums
                act.wait_ge(a_in[c], (g + 1) * PER_LOAD)
                if g >= 2:
                    act.wait_ge(deg_mm, g - 1)
                for m in range(QD * U):
                    if n_sums + m >= U:
                        act.wait_ge(junk_written, n_sums + m - U + 1)
                    act.activation(junk[(m // 2) % 2][:, m % 2 * CHUNK_COLS:(m % 2 + 1) * CHUNK_COLS], araw[:, c, m], ACT.Copy,
                                   accum_out=part[:, g % 2, c, m:m + 1]).then_inc(junk_written, 1)
                n_sums += QD * U
                act.wait_ge(junk_written, n_sums)
                act.nop().then_inc(part_act, 1)

            def ht_copy(g):
                act.wait_ge(ht_mm, g + 1)
                if g >= 1:
                    act.wait_ge(hw_mm, g)
                act.activation(flat(t_st[:]), ps_t, ACT.Copy).then_inc(ht_ev, 1)

            def hw_store(g):
                act.wait_ge(hw_mm, g + 1)
                if g >= 1:
                    act.wait_ge(z_out[(g - 1) % 2], ((g - 1) // 2 + 1) * QD * DMA)
                act.activation(flat(z_st[:]), ps_q, ACT.Copy).then_inc(hw_ev, 1)
                act.wait_ge(hw_ev, g + 1)
                for q in range(QD):
                    act.dma_start(hw_v[q, :, g], z_st[R * q:R * q + R]).then_inc(z_out[g % 2], DMA)

            def root(g):
                act.wait_ge(deg_done, g + 1)
                act.activation(root_deg[:], deg_g[:, g], ACT.Sqrt).then_inc(sqrt_done, 1)

            def keep_partial(g):
                act.wait_ge(diag_used, g + 1)
                act.activation(xs_m[g], by_block(acc[g % 2]), ACT.Copy).then_inc(acc_read, 1)

            for g in range(GROUPS):
                row_sums(g, 0)
                if g >= 1:
                    keep_partial(g - 1)
                ht_copy(g)
                if act_sums(g, 1):
                    row_sums(g, 1)
                if g == 0:
                    normalize(1)
                row_sums(g, 2)
                root(g)
                hw_store(g)
                if g + 2 < GROUPS:
                    normalize(g + 2)
            keep_partial(GROUPS - 1)

            def finish_first(k):
                g = F1[k]
                act.wait_ge(zt_mm, k + 1)
                act.activation(zt_hi_g[:, g], ps_t.rearrange("p (u q s) -> p u q s", u=U, q=QD), ACT.Copy)
                if k >= 1:
                    act.wait_ge(q_mm, k)
                act.activation(flat(t_st[:]), ps_t, ACT.Square).then_inc(zt_ev, 1)
                for u in range(U):
                    t = GROUPS * u + g
                    ins = act.activation(junk[0][:, u * F:u * F + F], z_st[:, u], ACT.Square, accum_out=nsq[:, t:t + 1])
                ins.then_inc(sq_done, 1)
                act.wait_ge(q_mm, k + 1)
                act.activation(sq_rows_g[0:R, g], ps_q[0:R].rearrange("p (u q s) -> p u q s", u=U, q=QD), ACT.Copy).then_inc(qh_done, 1)
                act.wait_ge(sq_done, k + 1)
                act.activation(flat(z_st[R:2 * R]).bitcast(F32R), ps_q[R:2 * R], ACT.Copy).then_inc(qh_done, 1)

            for k in range(GROUPS):
                finish_first(k)
            act.wait_ge(nsq_done, 1)

            def leave(it, par, pair):
                for c in range(4):
                    if c == 0 and not isinstance(pair, int):
                        if par:
                            act.wait_ge(max_done, pair)
                        else:
                            act.wait_ge(block_maxima, pair)
                            act.wait_ge(keys_out, pair * (4 * DMA))
                    wait_alone(act, bank_mm, it * 4 + (c + 1))
                    act.activation(keys[par][:, c * 1024:c * 1024 + 1024],
                                   ps[:, 2 * c:2 * c + 2].rearrange("p a b -> p (a b)"), ACT.Identity,
                                   bias=nsq[:, bass.ds(it, 1)], scale=2.0).then_inc(key_ev, 1)

            act.wait_ge(t_ready, UNITS1)
            for par in range(2):
                leave(par, par, 0)
            with act.Fori(1, TILES // 2) as pair:
                for par in range(2):
                    leave(pair * 2 + par, par, pair)
            vals_f = vals[:].rearrange("p t k -> p (t k)")
            act.wait_ge(s_arg, 1)
            act.activation(vals_f, vals_f, ACT.Sqrt).then_inc(s_root, 1)
            act.wait_ge(s_root, 1)
            act.activation(vals_f, vals_f, ACT.Exp, scale=-0.5).then_inc(s_exp, 1)
            act.wait_ge(deg2, 1)
            act.activation(tmp32[:], tmp32[:], ACT.Sqrt).then_inc(deg2_root, 1)

            def evacuate(g, bank, base_unit, base_z):
                act.wait_ge(t_used, g * GROUPS + (base_unit + GROUPS))
                act.wait_ge(z_mm, g + base_z)
                act.wait_ge(z_done, g + base_z)
                act.activation(out_t_m, by_block(acc[bank]), ACT.Copy).then_inc(acc_read, 1)

            def finish_second(g):
                act.wait_ge(var_ready, g + 2)
                act.activation(tmp32[:, 0:U], tmp32[:, 0:U], ACT.Sqrt).then_inc(sd_done, 1)
                act.wait_ge(kept, g + 1)
                act.wait_ge(zt_mm, g + GROUPS)
                wait_alone(act, z_done, g + (GROUPS + 1))
                for u in range(U):
                    ins = act.activation(z_st[:, u], xs[:, bass.ds(g + GROUPS * u, 1), :].rearrange("p o f -> p (o f)"), ACT.Relu,
                                         bias=negmr[:, u:u + 1], scale=tmp32[:, u:u + 1])
                ins.then_inc(h2_done, 1)
                act.wait_ge(zt_mm, g + (GROUPS + 1))
                act.wait_ge(q_mm, g + GROUPS)
                act.activation(flat(t_st[:]), ps_t, ACT.Copy).then_inc(zt_ev, 1)

            evacuate(0, 0, USED1, GROUPS)
            finish_second(0)
            evacuate(1, 1, USED1, GROUPS)
            with act.Fori(1, GROUPS // 2) as pair:
                for i in range(2):
                    finish_second(pair * 2 + (i - 1))
                    evacuate(pair * 2 + i, i, USED1, GROUPS)
            finish_second(GROUPS - 1)

            def store(g, i):
                act.wait_ge(z_done, g + (2 * GROUPS + 1))
                src = (z_st, t_st)[i]
                for q in range(QD):
                    dst = out_v[q, :, g] if isinstance(g, int) else out_v[q, :, bass.ds(g, 1)].rearrange("s o u f -> s (o u) f")
                    act.dma_start(dst, src[R * q:R * q + R]).then_inc(z_out[i], DMA)

            def split_high(g, j):
                act.wait_ge(t_used, g * GROUPS + (USED1 + UNITS + j - 3))
                wait_alone(act, t_ready, g * GROUPS + (UNITS1 + UNITS + j + 1))
                act.activation(tr_hi[:, j // 2 % 2], tr[:, j % TSLOTS], ACT.Copy).then_inc(hi_done, 1)

            def group_third(g, i):
                split_high(g, 0)
                split_high(g, 2)
                evacuate(g - 1, 1 - i, USED1 + UNITS, 2 * GROUPS)
                split_high(g, 4)
                store(g - 1, 1 - i)
                split_high(g, 6)

            act.wait_ge(gath_used, GROUPS)
            group_third(1, 1)
            with act.Fori(1, GROUPS // 2) as pair:
                for i in range(2):
                    group_third(pair * 2 + i, i)
            evacuate(GROUPS - 1, 1, USED1 + UNITS, 2 * GROUPS)
            store(GROUPS - 1, 1)

        @block.vector
        def _(v):
            count = [0]

            def link(ins):
                count[0] += 1
                ins.then_inc(chained, 1)
                v.wait_ge(chained, count[0])

            v.memset(ident[:], 0.0).then_inc(const_st, 1)
            v.memset(fold[:], 0.0).then_inc(const_st, 1)
            v.memset(neghalf[:], -0.5).then_inc(const_st, 1)
            link(v.memset(pick[:].bitcast(F32), 0.0))
            v.memset(pick[0:1].bitcast(F32), 1.0)
            v.memset(pick[R:R + 1].bitcast(F32), 1.0)
            v.memset(sq_rows[2 * R:P].bitcast(F32), 0.0)
            v.wait_ge(x_in, QD * DMA)
            for t in range(TILES):
                ins = v.bn_stats(out=stats[:, t], in_=xs[:, t])
            link(ins)
            for t in range(TILES):
                ins = v.bn_aggr(out=mv[:, t], in_=stats[:, t])
            link(ins)
            v.tensor_scalar(tmp32[:], mv[:, :, 1], LN_EPS, None, ALU.add).then_inc(var_ready, 1)
            v.wait_ge(sqrt_done, 1)
            link(v.reciprocal(tmp32[:], tmp32[:]))
            v.scalar_tensor_tensor(negmr[:], mv[:, :, 0], -1.0, tmp32[:], ALU.mult, ALU.mult).then_inc(ln_ready, 1)

            def transposed(out, slot, off, tiles):
                src = araw[:, slot, :, off:off + tiles * R].rearrange("p m (t s) -> p t m s", s=R)
                return v.transpose(out.rearrange("p t (m s) -> p t m s", s=R), src)

            k = 0

            def unit(slot, first, tiles):
                nonlocal k
                if k + tiles > RING1:
                    v.wait_ge(t_used, k + tiles - RING1)
                transposed(ring1[:, k % RING1:k % RING1 + tiles], slot, first * R, tiles).then_inc(t_ready, 1)
                k += tiles

            def make_y(g):
                v.wait_ge(sqrt_done, g + 2)
                link(v.reciprocal(dinv_g[:, g], root_deg[:]))
                v.wait_ge(h_done, (g + 1) * U)
                v.tensor_tensor(ys_g[:, g], hs_g[:, g], dinv_g[:, g].unsqueeze(2).broadcast_to([P, U, F]), ALU.mult)\
                    .then_inc(y_ready, 1)

            n_sums = 0
            for n, (g, c, pieces) in enumerate(part_a):
                def sums():
                    nonlocal n_sums
                    if g >= 2:
                        v.wait_ge(deg_mm, g - 1)
                    v.tensor_reduce(part[:, g % 2, c], araw[:, c], axis=AX_X, op=ALU.add).then_inc(part_dve, 1)
                    n_sums += 1

                v.wait_ge(a_in[c], (g + 1) * PER_LOAD)
                if not act_sums(g, c):
                    sums()
                for p, (first, tiles) in enumerate(pieces):
                    if not late_diag(g - 1, c, p):
                        continue
                    unit(c, first, tiles)
                    make_y(g - 1)
                for p, (first, tiles) in enumerate(pieces):
                    if not late_diag(g - 1, c, p):
                        unit(c, first, tiles)
                if c == 0 and g >= 1:
                    v.wait_ge(diag_used, g)
                transposed(tr[:, TSLOTS - 1, c:c + 1], c, g * R, 1).then_inc(diag_ready, 1)
                if c == CHUNKS - 1:
                    v.wait_ge(deg_mm, g + 1)
                    for q in range(QD):
                        ins = v.tensor_copy(deg_g[R * q:R * q + R, g], ps_d[R * q:R * q + R, q * U:q * U + U])
                    ins.then_inc(deg_done, 1)
                    if not LATE[g]:
                        make_y(g)

            def add_partial(k_f):
                g = F1[k_f]
                v.wait_ge(t_used, TILES_A + ends[k_f])
                v.tensor_tensor(xs_m[g], by_block(acc[(GROUPS + k_f - 1) % 2]), xs_m[g], ALU.add).then_inc(acc_read, 1)

            def make_z(k_f):
                g = F1[k_f]
                v.wait_ge(z_mm, k_f + 1)
                if k_f >= 1:
                    v.wait_ge(q_done, k_f)
                    v.wait_ge(zt_mm, k_f)
                    v.wait_ge(sq_done, k_f)
                else:
                    for p in range(2):
                        v.wait_ge(z_out[p], GROUPS // 2 * QD * DMA)
                    v.wait_ge(bias_in, DMA)
                for u in range(U):
                    t = GROUPS * u + g
                    ins = v.scalar_tensor_tensor(z_st[:, u], ps_z[:, u * F:u * F + F], dinv[:, t:t + 1], bias[:], ALU.mult, ALU.add)
                link(ins)
                v.scalar_tensor_tensor(z_st[:], z_st[:], 0.1, z_st[:], ALU.mult, ALU.max).then_inc(z_done, 1)

            def split_z(k_f):
                g = F1[k_f]
                v.wait_ge(zt_ev, k_f + 1)
                v.tensor_tensor(zt_lo_g[:, g], ps_t.rearrange("p (u q s) -> p u q s", u=U, q=QD),
                                zt_hi_g[:, g].bitcast(F32), ALU.subtract).then_inc(zl_done, 1)

            def split_sq(k_f):
                g = F1[k_f]
                v.wait_ge(qh_done, 2 * k_f + 2)
                v.tensor_tensor(sq_rows_g[R:2 * R, g], ps_q[R:2 * R].rearrange("p (u q s) -> p u q s", u=U, q=QD),
                                z_st[R:2 * R].rearrange("p u (q s) -> p u q s", s=R), ALU.subtract).then_inc(q_done, 1)

            def stages(before, after):
                for k_f in range(GROUPS):
                    if before < SPLIT_Z[k_f] <= after:
                        split_z(k_f)
                    if before < SPLIT_SQ[k_f] <= after:
                        split_sq(k_f)
                    if k_f + 1 < GROUPS and before < ADD[k_f + 1] <= after:
                        add_partial(k_f + 1)
                    if before < MAKE_Z[k_f] <= after:
                        make_z(k_f)

            for n, (g, chunks, loaded, pieces) in enumerate(part_b):
                slot = (LOADS_A + n) % SLOTS
                v.wait_ge(a_in[slot], arrived[LOADS_A + n])
                for i in range(len(chunks)):
                    for first, tiles in pieces[i]:
                        unit(slot, i * loaded + first - (GROUPS - loaded), tiles)
                        stages(k - TILES_A - tiles, k - TILES_A)
            for t in range(USED1 - TILES_A, SPLIT_SQ[-1]):
                stages(t, t + 1)
            v.wait_ge(sq_done, GROUPS)
            v.tensor_scalar(nsq[:], nsq[:], -1.0, None, ALU.mult).then_inc(nsq_done, 1)

            v.max(m8[:, 0], ident[:]).then_inc(lane_max, 1)
            v.wait_ge(lane_max, 1)
            v.max_index(i8[:, 0], m8[:, 0], ident[:]).then_inc(lane_found, 1)
            v.wait_ge(lane_found, 1)
            link(v.tensor_scalar(lane_rows[:], i8[:, 0, 0:1], float(TILES), None, ALU.mult))

            def search_blocks(it, pair):
                key_blocks = keys[0].rearrange("p (b f) -> p b f", f=F)
                if isinstance(pair, int):
                    for c in range(4):
                        v.wait_ge(key_ev, c + 1)
                        ins = v.tensor_reduce(bmax[:, c * GROUPS:(c + 1) * GROUPS], key_blocks[:, c * GROUPS:(c + 1) * GROUPS],
                                              axis=AX_X, op=ALU.max)
                    ins.then_inc(block_maxima, 1)
                else:
                    wait_alone(v, key_ev, it * 4 + 4)
                    v.tensor_reduce(bmax[:], key_blocks, axis=AX_X, op=ALU.max).then_inc(block_maxima, 1)
                wait_alone(v, block_maxima, pair + 1)
                v.max(bm8[:], bmax[:]).then_inc(best_blocks, 1)
                if not isinstance(pair, int):
                    wait_alone(v, blocks_kept, pair)
                wait_alone(v, best_blocks, pair + 1)
                v.max_index(bi8[:], bm8[:], bmax[:]).then_inc(block_places, 1)

            def search(it, pair):
                if not isinstance(pair, int):
                    v.wait_ge(top_kept, pair * 4)
                wait_alone(v, key_ev, it * 4 + 4)
                v.max(m8[:, 1], keys[1]).then_inc(chained, 1)
                wait_alone(v, chained, pair + (count[0] + 1))
                v.max_index(i8[:, 1], m8[:, 1], keys[1]).then_inc(max_done, 1)

            def search_candidates(pair):
                wait_alone(v, cand_in, pair * CAND + CAND)
                v.max(m8[:, 0], cand_f).then_inc(cand_max, 1)
                wait_alone(v, cand_max, pair + 1)
                v.max_index(i8[:, 0], m8[:, 0], cand_f).then_inc(cand_used, 1)

            def search_pair(pair):
                search_blocks(pair * 2, pair)
                search(pair * 2 + 1, pair)
                search_candidates(pair)

            search_pair(0)
            with v.Fori(1, TILES // 2) as pair:
                search_pair(pair)
            count[0] += TILES // 2
            vals_f = vals[:].rearrange("p t k -> p (t k)")
            v.wait_ge(top_kept, 2 * TILES)
            link(v.tensor_scalar(vals_f, vals_f, -1.0, 0.0, ALU.mult, ALU.max))
            v.tensor_scalar(vals_f, vals_f, 1e-10, None, ALU.add).then_inc(s_arg, 1)

            def product_unit(g, j, base_group, base_unit, place=None, slot_split=None):
                place = j if place is None else place
                c, half = divmod(j, CHUNK_UNITS)
                if half == 0:
                    v.wait_ge(a_in[c], (g + base_group + 1) * PER_LOAD + loads_in[c])
                if slot_split is not None:
                    v.wait_ge(lo_done, slot_split)
                else:
                    v.wait_ge(t_used, g * GROUPS + (base_unit + place - TSLOTS + 1))
                transposed(tr[:, place % TSLOTS], c, half * UNIT_COLS, U).then_inc(t_ready, 1)

            for j in range(2):
                product_unit(0, j, 0, USED1)
            v.wait_ge(s_exp, 1)
            link(v.tensor_reduce(tmp32[:], vals[:], axis=AX_X, op=ALU.add))
            v.tensor_tensor(tmp32[:], tmp32[:], deg[:], ALU.add).then_inc(deg2, 1)
            v.wait_ge(deg2_root, 1)
            link(v.reciprocal(dinv[:], tmp32[:]))
            for j in range(GROUPS):
                sl = slice(j * U, j * U + U)
                v.tensor_tensor(ys[:, sl], hs[:, sl], dinv[:, sl].unsqueeze(2).broadcast_to([P, U, F]), ALU.mult).then_inc(y_ready, 1)
            v.wait_ge(y_ready, 2 * GROUPS)
            v.wait_ge(hw_in, QD * DMA)
            v.tensor_tensor(hs[:], hw_sb, dinv[:].unsqueeze(2).broadcast_to([P, TILES, F]), ALU.mult).then_inc(gw_ready, 1)
            v.wait_ge(gw_ready, 1)

            base2 = count[0]
            PER_FINISH2 = TOPK - 1

            def finish_second_a(g, i):
                v.wait_ge(z_mm, g + (GROUPS + 1))
                v.wait_ge(gath_in[i], (g - i) * (GATHER // 2) + GATHER)
                for kk in range(TOPK):
                    for u in range(U):
                        s_k = vals[:, bass.ds(g + GROUPS * u, 1), kk:kk + 1].rearrange("p o k -> p (o k)")
                        own = out_t[:, u * F:u * F + F]
                        before = ps_z[:, u * F:u * F + F] if kk == 0 else own
                        ins = v.scalar_tensor_tensor(own, gath[:, i, u, kk], s_k, before, ALU.mult, ALU.add)
                    if kk < TOPK - 1:
                        ins.then_inc(chained, 1)
                        v.wait_ge(chained, g * PER_FINISH2 + (base2 + kk + 1))
                ins.then_inc(gath_used, 1)
                v.wait_ge(gath_used, g + 1)
                for u in range(U):
                    x_u = xs[:, bass.ds(g + GROUPS * u, 1), :].rearrange("p o f -> p (o f)")
                    ins = v.scalar_tensor_tensor(x_u, out_t[:, u * F:u * F + F], dinv[:, bass.ds(g + GROUPS * u, 1)], x_u, ALU.mult, ALU.add)
                ins.then_inc(x1_done, 1)
                wait_alone(v, x1_done, g + 1)
                for u in range(U):
                    ins = v.bn_stats(out=stats4[:, u], in_=xs[:, bass.ds(g + GROUPS * u, 1), :].rearrange("p o f -> p (o f)"))
                ins.then_inc(stats_done, 1)
                wait_alone(v, stats_done, g + 1)
                for u in range(U):
                    ins = v.bn_aggr(out=mv[:, u], in_=stats4[:, u])
                ins.then_inc(aggr_done, 1)
                v.wait_ge(zt_ev, g + GROUPS)
                v.wait_ge(aggr_done, g + 1)
                v.tensor_scalar(tmp32[:, 0:U], mv[:, 0:U, 1], LN_EPS, None, ALU.add).then_inc(var_ready, 1)

            def finish_second_b(g):
                v.wait_ge(sd_done, g + 1)
                v.reciprocal(tmp32[:, 0:U], tmp32[:, 0:U]).then_inc(rsd_done, 1)
                v.wait_ge(rsd_done, g + 1)
                v.scalar_tensor_tensor(negmr[:, 0:U], mv[:, 0:U, 0], -1.0, tmp32[:, 0:U], ALU.mult, ALU.mult).then_inc(z_done, 1)

            def finish_second_c(g):
                v.wait_ge(xb_ready, g + 1)
                v.wait_ge(q_mm, g + (GROUPS + 1))
                x_g = xs_g[:, g] if isinstance(g, int) else xs_g[:, bass.ds(g, 1)].rearrange("p o u f -> p (o u) f")
                v.tensor_tensor(x_g, ps_q.rearrange("p (u f) -> p u f", u=U), x_g, ALU.add).then_inc(q_done, 1)

            def group_second(g, i, prev, before, first=0):
                for j in range(first, GROUPS):
                    product_unit(g, j, 0, USED1)
                    if j == 3 and before is not None:
                        finish_second_c(before)
                    if prev is not None:
                        if j == 6:
                            finish_second_a(prev, 1 - i)
                        if j == 7:
                            finish_second_b(prev)

            def finish_third(g, i):
                v.wait_ge(z_mm, g + (2 * GROUPS + 1))
                if isinstance(g, int):
                    src = xs_g[:, g]
                    v.wait_ge(z_out[i], GROUPS // 2 * QD * DMA)
                else:
                    src = xs_g[:, bass.ds(g, 1)].rearrange("p o u f -> p (o u) f")
                    v.wait_ge(z_out[i], (g - i) * (QD * DMA // 2) + GROUPS // 2 * QD * DMA)
                v.tensor_tensor((z_st, t_st)[i][:], ps_z.rearrange("p (u f) -> p u f", u=U), src, ALU.add).then_inc(z_done, 1)

            def group_third(g, i, prev):
                for j in range(GROUPS):
                    after_split = j % 2 == 0 and not (isinstance(g, int) and j < TSLOTS)
                    product_unit(g, j, GROUPS, USED1 + UNITS, slot_split=split_units(g, j) - 1 if after_split else None)
                    if j == 2 and isinstance(g, int):
                        finish_second_c(GROUPS - 1)
                    if j == 3:
                        finish_third(prev, 1 - i)

            group_second(0, 0, None, None, first=2)
            group_second(1, 1, 0, None)
            with v.Fori(1, GROUPS // 2) as pair:
                for i in range(2):
                    group_second(pair * 2 + i, i, pair * 2 + (i - 1), pair * 2 + (i - 2))
            for place, j in enumerate(EVENS_FIRST):
                product_unit(0, j, GROUPS, USED1 + UNITS, place)
                if place == TSLOTS - 1:
                    finish_second_a(GROUPS - 1, 1)
                    finish_second_b(GROUPS - 1)
                    finish_second_c(GROUPS - 2)
            group_third(1, 1, 0)
            with v.Fori(1, GROUPS // 2) as pair:
                for i in range(2):
                    group_third(pair * 2 + i, i, pair * 2 + (i - 1))
            v.wait_ge(z_mm, 3 * GROUPS)
            v.wait_ge(z_out[1], (GROUPS - 1) * QD * DMA)
            v.tensor_tensor(t_st[:], ps_z.rearrange("p (u f) -> p u f", u=U), xs_g[:, GROUPS - 1], ALU.add).then_inc(z_done, 1)

        @block.tensor
        def _(pe):
            pe.wait_ge(consts, CONSTS)
            pe.wait_ge(w_in, 3 * DMA)
            pe.transpose(ps_z[:, 0:F], w_raw[:, 0:F], ident[:])
            pe.transpose(ps_z[:, F:2 * F], w_raw[:, F:2 * F], ident[:]).then_inc(wt_mm, 1)

            def four(dst, lhs, rhs):
                for u in range(U):
                    ins = pe.matmul(dst[:, u * F:u * F + F], lhs[:, u * P:u * P + P], rhs, start=True, stop=True)
                return ins

            def transposes(dst, src):
                for u in range(U):
                    ins = pe.transpose(dst[:, u * F:u * F + F], src(u), ident[:])
                return ins

            def first_unit(c, first, tiles, bank, start, stop):
                nonlocal k, n_pieces
                n_pieces += 1
                pe.wait_ge(t_ready, n_pieces)
                for i in range(tiles):
                    pe.matmul(acc[bank], ys[:, c * GROUPS + first + i], ring1[:, (k + i) % RING1],
                              start=start and i == 0, stop=stop and i == tiles - 1).then_inc(t_used, 1)
                k += tiles

            def diagonal(g):
                pe.wait_ge(diag_ready, (g + 1) * CHUNKS)
                pe.wait_ge(y_ready, g + 1)
                for cc in range(CHUNKS):
                    ins = pe.matmul(acc[g % 2], ys[:, cc * GROUPS + g], tr[:, TSLOTS - 1, cc],
                                    start=g == 0 and cc == 0, stop=cc == CHUNKS - 1)
                ins.then_inc(diag_used, 1)

            k = n_pieces = 0
            for n, (g, c, pieces) in enumerate(part_a):
                if c == 0:
                    pe.wait_ge(h_done, (g + 1) * U)
                    if g >= 1:
                        pe.wait_ge(ht_ev, g)
                    transposes(ps_t, lambda u: hs[:, GROUPS * u + g]).then_inc(ht_mm, 1)
                    if g >= 2:
                        pe.wait_ge(acc_read, g - 1)
                if c == CHUNKS - 1:
                    pe.wait_ge(ht_ev, g + 1)
                    if g >= 1:
                        pe.wait_ge(hw_ev, g)
                    four(ps_q, flat(t_st[:]), w2s[:]).then_inc(hw_mm, 1)
                    pe.wait_ge(part_dve, consumed[n][2])
                    pe.wait_ge(part_act, consumed[n][3])
                    if g >= 1:
                        pe.wait_ge(deg_done, g)
                    for cc in range(CHUNKS):
                        ins = pe.matmul(ps_d[:, 0:U * QD], fold[:], part[:, g % 2, cc], start=cc == 0, stop=cc == CHUNKS - 1)
                    ins.then_inc(deg_mm, 1)
                for p, (first, tiles) in enumerate(pieces):
                    first_unit(c, first, tiles, g % 2, c == 0 and p == 0, False)
                    if late_diag(g - 1, c, p):
                        diagonal(g - 1)
                if c == CHUNKS - 1 and not LATE[g]:
                    diagonal(g)

            def finish_first_a(k_f):
                pe.wait_ge(acc_read, GROUPS + k_f)
                if k_f >= 1:
                    pe.wait_ge(z_done, k_f)
                for u in range(U):
                    ins = pe.matmul(ps_z[:, u * F:u * F + F], xs_g[:, F1[k_f], u], w1s[:], start=True, stop=True)
                ins.then_inc(z_mm, 1)

            def finish_first_b(k_f):
                pe.wait_ge(z_done, k_f + 1)
                if k_f >= 1:
                    pe.wait_ge(zl_done, k_f)
                transposes(ps_t, lambda u: z_st[:, u]).then_inc(zt_mm, 1)

            def finish_first_c(k_f):
                pe.wait_ge(zt_ev, k_f + 1)
                if k_f >= 1:
                    pe.wait_ge(q_done, k_f)
                pe.matmul(ps_q, neghalf[:], flat(t_st[:]), start=True, stop=True).then_inc(q_mm, 1)

            def stages(before, after):
                for k_f in range(GROUPS):
                    if before < STAGE_B[k_f] <= after:
                        finish_first_b(k_f)
                    if before < STAGE_C[k_f] <= after:
                        finish_first_c(k_f)
                    if before < STAGE_A[k_f] <= after:
                        finish_first_a(k_f)

            for g, chunks, _, pieces in part_b:
                j = GROUPS - 2 - g
                if chunks[0] == 0:
                    pe.wait_ge(acc_read, GROUPS + j - 1)
                for c, of_chunk in zip(chunks, pieces):
                    for first, tiles in of_chunk:
                        first_unit(c, first, tiles, (GROUPS + j) % 2, c == 0 and first == g + 1,
                                   c == CHUNKS - 1 and first + tiles == GROUPS)
                        stages(k - TILES_A - tiles, k - TILES_A)
            for t in range(USED1 - TILES_A, STAGE_C[-1]):
                stages(t, t + 1)

            def distances(it, par):
                pe.wait_ge(zs_ready, it * 2 + 2)
                for c in range(8):
                    cols = slice(c * 512, c * 512 + 512)
                    if c % 2 == 0 and not (isinstance(it, int) and it < 1):
                        pe.wait_ge(key_ev, it * 4 + (c // 2 - 3))
                    zh = zt_hi[:].rearrange("p q t s -> p (q t s)")[:, cols]
                    zl = zt_lo[:].rearrange("p q t s -> p (q t s)")[:, cols]
                    sq = sq_rows[:].rearrange("p q t s -> p (q t s)")[:, cols]
                    pe.matmul(ps[:, c], pick[:], sq, start=True, stop=False)
                    pe.matmul(ps[:, c], zs_hi[:, par], zl, start=False, stop=False)
                    pe.matmul(ps[:, c], zs_lo[:, par], zh, start=False, stop=False)
                    ins = pe.matmul(ps[:, c], zs_hi[:, par], zh, start=False, stop=True)
                    if c % 2:
                        ins.then_inc(bank_mm, 1)

            pe.wait_ge(q_done, GROUPS)
            for par in range(2):
                distances(par, par)
            with pe.Fori(1, TILES // 2) as pair:
                for par in range(2):
                    distances(pair * 2 + par, par)

            def unit(g, j, bank, base_unit, src):
                pe.wait_ge(t_ready, g * GROUPS + (base_unit + j + 1))
                for i in range(U):
                    ins = pe.matmul(acc[bank], src[:, j * U + i], tr[:, j % TSLOTS, i],
                                    start=j == 0 and i == 0, stop=j == GROUPS - 1 and i == U - 1)
                ins.then_inc(t_used, 1)

            def finish_second_a(g):
                pe.wait_ge(acc_read, g + 2 * GROUPS)
                pe.wait_ge(z_done, g + GROUPS)
                four(ps_z, out_t[:], w2s[:]).then_inc(z_mm, 1)

            def finish_second_b(g):
                pe.wait_ge(h2_done, g + 1)
                pe.wait_ge(zt_ev, g + GROUPS)
                transposes(ps_t, lambda u: z_st[:, u]).then_inc(zt_mm, 1)

            def finish_second_c(g):
                pe.wait_ge(zt_ev, g + (GROUPS + 1))
                pe.wait_ge(q_done, g + GROUPS)
                four(ps_q, flat(t_st[:]), ws_t[:]).then_inc(q_mm, 1)

            def group_second(g, i, prev, before):
                pe.wait_ge(acc_read, g + (2 * GROUPS - 2))
                for j in range(GROUPS):
                    if isinstance(g, int) and g == 0:
                        pe.wait_ge(y_ready, GROUPS + j + 1)
                    unit(g, j, i, UNITS1, ys)
                    if j == 0 and before is not None:
                        finish_second_b(before)
                    if j == 1 and before is not None:
                        finish_second_c(before)
                    if j == 2 and prev is not None:
                        finish_second_a(prev)

            def split_unit(g, j, bank):
                pe.wait_ge(lo_done, split_units(g, j) + 1)
                half = j // 2 % 2
                for i in range(U):
                    for n, (y, t) in enumerate(((y_hi, tr_lo), (y_lo, tr_hi), (y_hi, tr_hi))):
                        ins = pe.matmul(acc[bank], y[:, i, j // 2], t[:, half, i],
                                        start=j == 0 and i == 0 and n == 0, stop=False)
                ins.then_inc(t_used, 1)

            def finish_third(g):
                pe.wait_ge(acc_read, g + 3 * GROUPS)
                pe.wait_ge(z_done, g + 2 * GROUPS)
                four(ps_z, out_t[:], wn_t[:]).then_inc(z_mm, 1)

            def group_third(g, i, prev):
                pe.wait_ge(acc_read, g + (3 * GROUPS - 2))
                for j in range(GROUPS):
                    if j % 2 == 0:
                        split_unit(g, j, i)
                    else:
                        unit(g, j, i, UNITS1 + UNITS, hs)
                    if prev is not None and j == 0:
                        finish_third(prev)

            pe.wait_ge(key_ev, 4 * TILES)
            pe.wait_ge(wt_ev, 2)
            group_second(0, 0, None, None)
            group_second(1, 1, 0, None)
            with pe.Fori(1, GROUPS // 2) as pair:
                for i in range(2):
                    group_second(pair * 2 + i, i, pair * 2 + (i - 1), pair * 2 + (i - 2))
            pe.wait_ge(acc_read, 3 * GROUPS - 2)
            finish_second_b(GROUPS - 2)
            for place, j in enumerate(EVENS_FIRST):
                pe.wait_ge(t_ready, UNITS1 + UNITS + place + 1)
                for i in range(U):
                    if place in (0, TSLOTS):
                        pe.wait_ge(kept, j % 2 * U + i + 2)
                    ins = pe.matmul(acc[0], hs[:, j * U + i], tr[:, place % TSLOTS, i],
                                    start=place == 0 and i == 0, stop=place == GROUPS - 1 and i == U - 1)
                ins.then_inc(t_used, 1)
                if place == 0:
                    finish_second_c(GROUPS - 2)
                    finish_second_a(GROUPS - 1)
                if place == TSLOTS + 1:
                    finish_second_b(GROUPS - 1)
            finish_second_c(GROUPS - 1)
            pe.wait_ge(y_lo_done, U)
            group_third(1, 1, 0)
            with pe.Fori(1, GROUPS // 2) as pair:
                for i in range(2):
                    group_third(pair * 2 + i, i, pair * 2 + (i - 1))
            finish_third(GROUPS - 1)


_INS = ['x', 'adj', 'L0_gnn_W1', 'L0_gnn_b1', 'L0_gnn_W2', 'L0_gnn_b2', 'L1_gnn_W', 'L1_gnn_b']
_OUTS = [((N, F), 'float32')]


def kernel(**inputs):
    import numpy as _np
    import concourse.bacc as _bacc
    from concourse import mybir as _mybir
    from concourse.bass_utils import run_bass_kernel_spmd as _run

    nc = _bacc.Bacc("TRN2", target_bir_lowering=False, num_devices=1)
    arrays, args = {}, []
    for name in _INS:
        a = _np.ascontiguousarray(inputs[name])
        arrays[f"in_{name}_dram"] = a
        args.append(nc.dram_tensor(f"in_{name}_dram", a.shape, _mybir.dt.from_np(a.dtype), kind="ExternalInput").ap())
    for i, (shape, dtype) in enumerate(_OUTS):
        args.append(nc.dram_tensor(f"out_{i}_dram", shape, _mybir.dt.from_np(_np.dtype(dtype)), kind="ExternalOutput").ap())
    gnn_kernel(nc, *args)
    r = _run(nc, [arrays], core_ids=[0])
    return r.results[0]["out_0_dram"]
```
